# Optimizing a Trainium2 kernel written in Bass

```python
import numpy as np
import jax
import jax.numpy as jnp

def _softmax(x, axis=-1):
    return jax.nn.softmax(x, axis=axis)

def _gelu(x):
    return jax.nn.gelu(x, approximate=True)

def _silu(x):
    return jax.nn.silu(x)

def _sigmoid(x):
    return jax.nn.sigmoid(x)

def _layernorm(x, axis=-1, eps=1e-05):
    m = jnp.mean(x, axis=axis, keepdims=True)
    v = jnp.var(x, axis=axis, keepdims=True)
    return (x - m) / jnp.sqrt(v + eps)

def _scatter_add(tgt, idx, src, axis=0):
    return tgt.at[idx].add(src)

def _segment_sum(src, seg, n):
    return jax.ops.segment_sum(src, seg, n)
kernel_name = 'mk_macaron_d1_jaxref_r4_d6113b'

def setup_inputs(seed: int=0):
    np.random.seed(seed)
    _w = jnp.asarray

    def _L0_attn_setup():
        import jax, jax.numpy as jnp
        import numpy as np
        B, N, DIM = (4, 256, 256)
        H, DH = (16, 64)
        NUM_MEM = 4
        TOPK = 64
        QK_SCALE = 10.0

        def l2norm(t, eps=1e-12):
            return t / jnp.clip(jnp.linalg.norm(t, axis=-1, keepdims=True), eps)
        key = jax.random.key(seed)
        ks = jax.random.split(key, 12)
        s = 0.02
        inp = {'x': jax.random.normal(ks[0], (B, N, DIM), dtype=jnp.float32), 'Wq': jax.random.normal(ks[1], (DIM, H * DH), dtype=jnp.float32) * s, 'Wk': jax.random.normal(ks[2], (DIM, H * DH), dtype=jnp.float32) * s, 'Wv': jax.random.normal(ks[3], (DIM, H * DH), dtype=jnp.float32) * s, 'W_pre_th': jax.random.normal(ks[4], (H, H), dtype=jnp.float32) * (1.0 / H) ** 0.5, 'W_post_th': jax.random.normal(ks[5], (H, H), dtype=jnp.float32) * (1.0 / H) ** 0.5, 'mem_k': jax.random.normal(ks[6], (H, NUM_MEM, DH), dtype=jnp.float32), 'mem_v': jax.random.normal(ks[7], (H, NUM_MEM, DH), dtype=jnp.float32), 'head_scale_params': jnp.ones((1, H, 1, 1), dtype=jnp.float32), 'Wg': jax.random.normal(ks[8], (DIM, H * DH), dtype=jnp.float32) * s, 'bg': jnp.ones((H * DH,), dtype=jnp.float32), 'Wo': jax.random.normal(ks[9], (H * DH, DIM), dtype=jnp.float32) * s}
        return inp
    _L0_attn_in = _L0_attn_setup()

    def _L0_ffn_setup():
        import jax, jax.numpy as jnp
        import numpy as np
        EPS = 1e-06
        LN_EPS = 1e-05

        def _absmean_core(W):
            gamma = jnp.mean(jnp.abs(W)) + EPS
            Ws = W / gamma
            Wq = jnp.sign(Ws) * jnp.minimum(jnp.round(jnp.abs(Ws)), 1.0)
            return (Wq, gamma)

        @jax.custom_vjp
        def absmean(W):
            return _absmean_core(W)[0]

        def _absmean_fwd(W):
            Wq, gamma = _absmean_core(W)
            return (Wq, gamma)

        def _absmean_bwd(gamma, g):
            return (g / gamma,)
        absmean.defvjp(_absmean_fwd, _absmean_bwd)

        def layernorm(x, w, b, eps=LN_EPS):
            mu = jnp.mean(x, axis=-1, keepdims=True)
            var = jnp.mean((x - mu) ** 2, axis=-1, keepdims=True)
            return (x - mu) * jax.lax.rsqrt(var + eps) * w + b
        key = jax.random.key(seed)
        k1, k2, k3 = jax.random.split(key, 3)
        d, h = (256, 1024)
        B, T = (8, 512)
        return {'x': jax.random.normal(k1, (B, T, d), jnp.float32), 'W_fc': jax.random.normal(k2, (h, d), jnp.float32), 'ln_w': jnp.ones((h,), jnp.float32), 'ln_b': jnp.zeros((h,), jnp.float32), 'W_proj': jax.random.normal(k3, (d, h), jnp.float32)}
    _L0_ffn_in = _L0_ffn_setup()
    _d = {'L0_attn_x': _L0_attn_in['x'], 'L0_attn_Wq': _L0_attn_in['Wq'], 'L0_attn_Wk': _L0_attn_in['Wk'], 'L0_attn_Wv': _L0_attn_in['Wv'], 'L0_attn_W_pre_th': _L0_attn_in['W_pre_th'], 'L0_attn_W_post_th': _L0_attn_in['W_post_th'], 'L0_attn_mem_k': _L0_attn_in['mem_k'], 'L0_attn_mem_v': _L0_attn_in['mem_v'], 'L0_attn_head_scale_params': _L0_attn_in['head_scale_params'], 'L0_attn_Wg': _L0_attn_in['Wg'], 'L0_attn_bg': _L0_attn_in['bg'], 'L0_attn_Wo': _L0_attn_in['Wo'], 'L0_ffn_W_fc': _L0_ffn_in['W_fc'], 'L0_ffn_ln_w': _L0_ffn_in['ln_w'], 'L0_ffn_ln_b': _L0_ffn_in['ln_b'], 'L0_ffn_W_proj': _L0_ffn_in['W_proj']}
    _x0 = _d['L0_attn_x']
    _d['L0_attn_x'] = jax.random.normal(jax.random.fold_in(jax.random.key(seed), 1), (4, 1024, 256), dtype=_x0.dtype)
    del _x0
    return _d

def reference(L0_attn_x, L0_attn_Wq, L0_attn_Wk, L0_attn_Wv, L0_attn_W_pre_th, L0_attn_W_post_th, L0_attn_mem_k, L0_attn_mem_v, L0_attn_head_scale_params, L0_attn_Wg, L0_attn_bg, L0_attn_Wo, L0_ffn_W_fc, L0_ffn_ln_w, L0_ffn_ln_b, L0_ffn_W_proj):

    def _L0_attn_ref(x, Wq, Wk, Wv, W_pre_th, W_post_th, mem_k, mem_v, head_scale_params, Wg, bg, Wo):
        import jax, jax.numpy as jnp
        import numpy as np
        B, N, DIM = (4, 256, 256)
        H, DH = (16, 64)
        NUM_MEM = 4
        TOPK = 64
        QK_SCALE = 10.0

        def l2norm(t, eps=1e-12):
            return t / jnp.clip(jnp.linalg.norm(t, axis=-1, keepdims=True), eps)
        b, n, _ = x.shape
        q = (x @ Wq).reshape(b, n, H, DH).transpose(0, 2, 1, 3)
        k = (x @ Wk).reshape(b, n, H, DH).transpose(0, 2, 1, 3)
        v = (x @ Wv).reshape(b, n, H, DH).transpose(0, 2, 1, 3)
        mk = jnp.broadcast_to(mem_k[None], (b, H, NUM_MEM, DH))
        mv = jnp.broadcast_to(mem_v[None], (b, H, NUM_MEM, DH))
        k = jnp.concatenate([mk, k], axis=2)
        v = jnp.concatenate([mv, v], axis=2)
        q = l2norm(q)
        k = l2norm(k)
        dots = jnp.einsum('bhid,bhjd->bhij', q, k) * QK_SCALE
        dots = jnp.einsum('hg,bgij->bhij', W_pre_th, dots)
        mask_value = -jnp.finfo(dots.dtype).max
        j = n + NUM_MEM
        col_pos = jnp.arange(j) - NUM_MEM
        causal = jnp.arange(n)[:, None] < col_pos[None, :]
        dots = jnp.where(causal[None, None], mask_value, dots)
        top = jax.lax.top_k(dots, TOPK)[0]
        vk = top[..., -1:]
        dots = jnp.where(dots < vk, mask_value, dots)
        attn = jax.nn.softmax(dots, axis=-1)
        attn = jnp.einsum('hg,bgij->bhij', W_post_th, attn)
        out = jnp.einsum('bhij,bhjd->bhid', attn, v)
        out = out * head_scale_params
        out = out.transpose(0, 2, 1, 3).reshape(b, n, H * DH)
        gates = x @ Wg + bg
        out = out * jax.nn.sigmoid(gates)
        return out @ Wo

    def _L0_ffn_ref(x, W_fc, ln_w, ln_b, W_proj):
        import jax, jax.numpy as jnp
        import numpy as np
        EPS = 1e-06
        LN_EPS = 1e-05

        def _absmean_core(W):
            gamma = jnp.mean(jnp.abs(W)) + EPS
            Ws = W / gamma
            Wq = jnp.sign(Ws) * jnp.minimum(jnp.round(jnp.abs(Ws)), 1.0)
            return (Wq, gamma)

        @jax.custom_vjp
        def absmean(W):
            return _absmean_core(W)[0]

        def _absmean_fwd(W):
            Wq, gamma = _absmean_core(W)
            return (Wq, gamma)

        def _absmean_bwd(gamma, g):
            return (g / gamma,)
        absmean.defvjp(_absmean_fwd, _absmean_bwd)

        def layernorm(x, w, b, eps=LN_EPS):
            mu = jnp.mean(x, axis=-1, keepdims=True)
            var = jnp.mean((x - mu) ** 2, axis=-1, keepdims=True)
            return (x - mu) * jax.lax.rsqrt(var + eps) * w + b
        h = jnp.einsum('btd,hd->bth', x, absmean(W_fc))
        h = jax.nn.gelu(h, approximate=False)
        h = layernorm(h, ln_w, ln_b)
        return jnp.einsum('bth,dh->btd', h, absmean(W_proj))
    x = L0_attn_x
    x = x + 0.5 * _L0_ffn_ref(_layernorm(x, axis=-1), L0_ffn_W_fc, L0_ffn_ln_w, L0_ffn_ln_b, L0_ffn_W_proj)
    x = x + _L0_attn_ref(_layernorm(x, axis=-1), L0_attn_Wq, L0_attn_Wk, L0_attn_Wv, L0_attn_W_pre_th, L0_attn_W_post_th, L0_attn_mem_k, L0_attn_mem_v, L0_attn_head_scale_params, L0_attn_Wg, L0_attn_bg, L0_attn_Wo)
    x = x + 0.5 * _L0_ffn_ref(_layernorm(x, axis=-1), L0_ffn_W_fc, L0_ffn_ln_w, L0_ffn_ln_b, L0_ffn_W_proj)
    return x

_drawn_inputs = setup_inputs


def setup_inputs(seed=0):
    import zlib

    import numpy as np

    out = dict(_drawn_inputs(seed))
    spreads = {'L0_attn_head_scale_params': (1.0, 0.6),
     'L0_attn_bg': (1.0, 0.6),
     'L0_ffn_ln_w': (1.0, 0.2),
     'L0_ffn_ln_b': (0.0, 0.1)}
    factors = {'L0_attn_Wq': 8.0,
     'L0_attn_Wk': 8.0,
     'L0_attn_Wv': 8.0,
     'L0_attn_W_pre_th': 8.0,
     'L0_attn_W_post_th': 8.0,
     'L0_attn_mem_k': 8.0,
     'L0_attn_mem_v': 8.0,
     'L0_attn_Wg': 8.0,
     'L0_attn_Wo': 8.0}
    for name, (base, spread) in spreads.items():
        noise = np.random.default_rng([zlib.crc32(name.encode()), seed]).standard_normal(out[name].shape)
        drawn = base * np.exp(spread * noise) if base else spread * noise
        out[name] = jnp.asarray(drawn.astype(out[name].dtype))
    for name, factor in factors.items():
        out[name] = (out[name] * factor).astype(out[name].dtype)
    return out
```

```python
import numpy as np
import concourse.bass as bass
import concourse.mybir as mybir
from contextlib import ExitStack

B, N, DIM = 4, 1024, 256
H, DH = 16, 64
MEM, TOPK = 4, 64
HID = 1024
P = 128
DC = DIM // P
FC = HID // P
HP = H // 2
INNER = H * DH
MACRO = 512
U = N // MACRO
TT = MACRO // P
IB = N // P
R8 = P // H
TPB = P // R8
TPH = TPB // 2
JW = MEM + N
LN_EPS = 1e-5
Q_EPS = 1e-6
L2_EPS = 1e-12
QK_SCALE = 10.0
NEG = float(np.finfo(np.float32).min)
DRING = 3
F32 = mybir.dt.float32
ALU = mybir.AluOpType
ACT = mybir.ActivationFunctionType


def width(ib):
    return MEM + P * (ib + 1)


def pieces(n):
    k = -(-n // 512)
    cuts = [n * i // k for i in range(k + 1)]
    return list(zip(cuts[:-1], cuts[1:]))


def semaphores(nc, ctx, prefix, names, keep=()):
    made = {name: [ctx.enter_context(nc.semaphore(f"{prefix}_{name}{i}")) for i in range(count)]
            for name, count in names.items()}
    rounds = [sem for name, sems in made.items() if name not in keep for sem in sems]
    ends = {name: ctx.enter_context(nc.semaphore(f"{prefix}_{name}")) for name in ("arrive", "go", "passed")}
    return {"rounds": rounds, **ends, **{name: sems if len(sems) > 1 else sems[0] for name, sems in made.items()}}


def end_round(s, eng, b, leader=False):
    eng.drain().then_inc(s["arrive"], 1)
    if leader:
        eng.wait_ge(s["arrive"], 5 * (b + 1))
        eng.sem_inc(s["passed"], 1)
        for sem in s["rounds"]:
            eng.sem_clear(sem)
        eng.sem_inc(s["go"], 1)
    eng.wait_ge(s["go"], b + 1)
    eng.sem_inc(s["passed"], 1)


def ffn_buffers(nc, ctx, tag):
    def sb(name, shape):
        return ctx.enter_context(nc.sbuf_tensor(f"{tag}_{name}", shape, F32))
    b = {}
    b["x"] = sb("x", [P, 2, TT, DIM])
    b["xn"] = sb("xn", [P, TT, DIM])
    b["xnT"] = sb("xnT", [P, DC, MACRO])
    b["gT"] = sb("gT", [P, FC, MACRO])
    b["g2T"] = sb("g2T", [P, FC, MACRO])
    b["bn"] = sb("bn", [P, TT, 6])
    b["mv"] = sb("mv", [P, TT, 2])
    b["std"] = sb("std", [P, TT])
    b["rstd"] = sb("rstd", [P, TT])
    b["st"] = sb("st", [P, TT, 2])
    b["nv"] = sb("nv", [P, TT])
    b["nmu"] = sb("nmu", [P, TT])
    b["hstd"] = sb("hstd", [P, TT])
    b["hrstd"] = sb("hrstd", [P, TT])
    b["t1"] = sb("t1", [P, TT, DIM])
    b["t2"] = sb("t2", [P, TT, DIM])
    return b


FFN_SEMS = dict(x_in=2, stat=1, std=1, xn=1, tr=1, xnT=1, hid=1, gelu=1, sq=1, g_used=1,
                out=1, hstat=1, hstd=1, res=1, stored=2, link=1)
QKV_SEMS = dict(proj=1, square=1, ssq=1, norm=1, qk=1, qk_st=2, gate=1, sig=1, gs=1, g_st=2, val=1, v_out=1,
                v_st=2)


def build(nc, x, Wq, Wk, Wv, pre_th, post_th, mem_kT, mem_v, hs_col, Wg, bg_col, Wo, WfcT, lnw_col, lnb_col, WpT,
          ident_c, blocks_c, delta_c, mask_c, out):
    qd = nc.dram_tensor("q_scratch", [B, P, HP, N], F32, kind="Internal").ap()
    kd = nc.dram_tensor("k_scratch", [B, P, HP, N], F32, kind="Internal").ap()
    gd = nc.dram_tensor("gate_scratch", [B, P, HP, N], F32, kind="Internal").ap()
    vd = nc.dram_tensor("v_scratch", [B, N, INNER], F32, kind="Internal").ap()
    x1d = nc.dram_tensor("x1_scratch", [B, N, DIM], F32, kind="Internal").ap()
    x2d = nc.dram_tensor("x2_scratch", [B, N, DIM], F32, kind="Internal").ap()
    sd = nc.dram_tensor("score_scratch", [2, H, P, JW], F32, kind="Internal").ap()

    with ExitStack() as top:
        def sb(name, shape):
            return top.enter_context(nc.sbuf_tensor(name, shape, F32))
        ps = [top.enter_context(nc.psum_tensor(f"bank{i}", [P, 512], F32)) for i in range(8)]
        ident = sb("ident", [P, P])
        blocks = sb("blocks", [P, P])
        ones = sb("ones", [P, P])
        Wfc = sb("Wfc", [P, DC, HID])
        Wp = sb("Wp", [P, FC, DIM + 1])
        Bsum = sb("Bsum", [P, DIM])
        Csum = sb("Csum", [P, DIM])
        eps = sb("eps", [P, 1])
        weights_setup(nc, ps, ident, blocks, ones, Wfc, Wp, Bsum, Csum, eps, ident_c, blocks_c, WfcT, WpT, lnw_col,
                      lnb_col)
        consts = (ps, ident, blocks, ones, Wfc, Wp, Bsum, Csum, eps)
        mkT = sb("mkT", [P, HP * MEM])
        token_stage(nc, consts, "a", x, x1d, qkv=(Wq, Wk, Wv, Wg, bg_col, hs_col, mem_kT, mkT, qd, kd, vd, gd))
        attention(nc, ps, mkT, qd, kd, gd, vd, x1d, x2d, sd, pre_th, post_th, mem_v, Wo, delta_c, mask_c)
        token_stage(nc, consts, "c", x2d, out, qkv=None)


def weights_setup(nc, ps, ident, blocks, ones, Wfc, Wp, Bsum, Csum, eps, ident_c, blocks_c, WfcT, WpT, lnw_col,
                  lnb_col):
    with ExitStack() as ctx:
        def sb(name, shape):
            return ctx.enter_context(nc.sbuf_tensor(name, shape, F32))
        raw = sb("w_raw", [P, 2, HID * DC])
        absw = sb("w_abs", [P, 2, HID * DC])
        asum = sb("w_asum", [P, 2])
        thr = sb("w_thr", [P, 2])
        nthr = sb("w_nthr", [P, 2])
        neg = sb("w_neg", [P, 2, HID * DC])
        tern = sb("w_tern", [P, HID * DC])
        wb = sb("w_b", [P, FC, DIM])
        lnw = sb("lnw", [P, FC])
        lnb = sb("lnb", [P, FC])
        s = semaphores(nc, ctx, "w", dict(load=1, asum=1, ones=1, tot=1, link=1, wp=1, sums=1))
        block = ctx.enter_context(nc.Block())

        @block.sync
        def _(sp):
            sp.dma_start(raw[:, 0, :].rearrange("p (c f) -> p c f", c=DC),
                         WfcT.rearrange("(c p) f -> p c f", p=P)).then_inc(s["load"], 16)
            sp.dma_start(raw[:, 1, :].rearrange("p (c f) -> p c f", c=FC),
                         WpT.rearrange("(c p) f -> p c f", p=P)).then_inc(s["load"], 16)
            sp.dma_start(lnw[:], lnw_col).then_inc(s["load"], 16)
            sp.dma_start(lnb[:], lnb_col).then_inc(s["load"], 16)
            sp.dma_start(ident[:], ident_c).then_inc(s["load"], 16)
            sp.dma_start(blocks[:], blocks_c).then_inc(s["load"], 16)

        @block.scalar
        def _(act):
            act.wait_ge(s["load"], 96)
            for i in range(2):
                nc.scalar.activation(absw[:, i, :], raw[:, i, :], ACT.Abs,
                                     accum_out=asum[:, i:i + 1]).then_inc(s["asum"], 1)

        @block.tensor
        def _(pe):
            pe.wait_ge(s["ones"], 1)
            pe.wait_ge(s["asum"], 2)
            nc.tensor.matmul(ps[0][:, 0:2], ones[:], asum[:], start=True, stop=True).then_inc(s["tot"], 1)
            pe.wait_ge(s["wp"], 2)
            for c in range(FC):
                nc.tensor.matmul(ps[1][:, 0:DIM], ones[:], Wp[:, c, 0:DIM], start=(c == 0), stop=(c == FC - 1))
            for c in range(FC):
                last = nc.tensor.matmul(ps[2][:, 0:DIM], ones[:], wb[:, c, :], start=(c == 0), stop=(c == FC - 1))
            last.then_inc(s["sums"], 1)

        @block.vector
        def _(dve):
            count = [0]

            def link(ins):
                count[0] += 1
                ins.then_inc(s["link"], 1)
                dve.wait_ge(s["link"], count[0])

            nc.vector.memset(eps[:], LN_EPS)
            nc.vector.memset(Wp[:, :, DIM:DIM + 1], 1.0)
            nc.vector.memset(ones[:], 1.0).then_inc(s["ones"], 1)
            dve.wait_ge(s["load"], 96)
            dve.wait_ge(s["tot"], 1)
            link(nc.vector.tensor_scalar(thr[:], ps[0][:, 0:2], 1.0 / (DIM * HID), Q_EPS, ALU.mult, ALU.add))
            link(nc.vector.tensor_scalar(nthr[:], thr[:], -0.5, None, ALU.mult))
            link(nc.vector.tensor_scalar(thr[:], thr[:], 0.5, None, ALU.mult))
            for i in range(2):
                link(nc.vector.tensor_scalar(neg[:, i, :], raw[:, i, :], nthr[:, i:i + 1], None, ALU.is_lt))
            nc.vector.scalar_tensor_tensor(out=Wfc[:].rearrange("p c f -> p (c f)"), in0=raw[:, 0, :],
                                           scalar=thr[:, 0:1], in1=neg[:, 0, :], op0=ALU.is_gt, op1=ALU.subtract)
            link(nc.vector.scalar_tensor_tensor(out=tern[:], in0=raw[:, 1, :], scalar=thr[:, 1:2], in1=neg[:, 1, :],
                                                op0=ALU.is_gt, op1=ALU.subtract))
            for c in range(FC):
                nc.vector.tensor_scalar(wb[:, c, :], tern[:, c * DIM:(c + 1) * DIM], lnb[:, c:c + 1], None, ALU.mult)
                last = nc.vector.tensor_scalar(Wp[:, c, 0:DIM], tern[:, c * DIM:(c + 1) * DIM], lnw[:, c:c + 1], None,
                                               ALU.mult)
            last.then_inc(s["wp"], 2)
            dve.wait_ge(s["sums"], 1)
            nc.vector.tensor_copy(Bsum[:], ps[1][:, 0:DIM])
            nc.vector.tensor_copy(Csum[:], ps[2][:, 0:DIM])


def token_stage(nc, consts, tag, src, dst, qkv):
    ps, ident, blocks, ones, Wfc, Wp, Bsum, Csum, eps = consts
    with ExitStack() as ctx:
        def sb(name, shape):
            return ctx.enter_context(nc.sbuf_tensor(name, shape, F32))
        f = ffn_buffers(nc, ctx, tag)
        X, xn, xnT, gT, g2T = f["x"], f["xn"], f["xnT"], f["gT"], f["g2T"]
        LNS = 2 if qkv else 1
        names = dict(FFN_SEMS)
        if qkv:
            names.update(QKV_SEMS)
            names.update(dict(w_in=1, memk=1, mem=1))
        s = semaphores(nc, ctx, tag, names, keep=("w_in", "memk", "mem"))
        if qkv:
            Wq_d, Wk_d, Wv_d, Wg_d, bg_col, hs_col, mem_kT, mkT, qd, kd, vd, gd = qkv
            W4 = sb("W4", [P, 4, DC, INNER])
            bg = sb("bg", [P, HP])
            hs = sb("hs", [P, HP])
            mraw = sb("mraw", [P, HP * MEM])
            msq = sb("msq", [P, HP * MEM])
            mrt = sb("mrt", [P, HP * MEM])
            sq = sb("sq", [P, 2, MACRO])
            rt = sb("rt", [P, 2, MACRO])
            rr = sb("rr", [P, 2, MACRO])
            ri = sb("ri", [P, 2, MACRO])
            qn = sb("qn", [P, 2, MACRO])
            sg = sb("sg", [P, 2, MACRO])
            gs = sb("gs", [P, 2, MACRO])
            vo = sb("vo", [P, 2, MACRO])
        QC = 2 * HP
        VC = TT * (INNER // 512)
        block = ctx.enter_context(nc.Block())

        @block.sync
        def _(sp):
            if qkv:
                for i, w in enumerate((Wq_d, Wk_d, Wv_d, Wg_d)):
                    sp.dma_start(W4[:, i, :, :], w.rearrange("(c p) n -> p c n", p=P)).then_inc(s["w_in"], 16)
                sp.dma_start(bg[:], bg_col).then_inc(s["w_in"], 16)
                sp.dma_start(hs[:], hs_col).then_inc(s["w_in"], 16)
                sp.dma_start(mraw[:], mem_kT).then_inc(s["w_in"], 16)
            with sp.Fori(0, B) as b:
                for u in range(U):
                    if u == 0:
                        for v in range(U):
                            sp.dma_start(X[:, v], src[b, v * MACRO:(v + 1) * MACRO].rearrange(
                                "(t p) d -> p t d", p=P)).then_inc(s["x_in"][v], 16)
                    sp.wait_ge(s["res"], (u + 1) * TT)
                    sp.dma_start(dst[b, u * MACRO:(u + 1) * MACRO].rearrange("(t p) d -> p t d", p=P),
                                 X[:, u]).then_inc(s["stored"][u], 16)
                    if qkv:
                        tok = slice(u * MACRO, (u + 1) * MACRO)
                        for c in range(QC):
                            sp.wait_ge(s["qk"], u * QC + c + 1)
                            sp.dma_start((qd if c < HP else kd)[b, :, c % HP, tok],
                                         qn[:, c % 2, :]).then_inc(s["qk_st"][c % 2], 16)
                        for c in range(HP):
                            sp.wait_ge(s["gs"], u * HP + c + 1)
                            sp.dma_start(gd[b, :, c, tok], gs[:, c % 2, :]).then_inc(s["g_st"][c % 2], 16)
                        for c in range(VC):
                            sp.wait_ge(s["v_out"], u * VC + c + 1)
                            t, h = c // 2, c % 2
                            sp.dma_start(vd[b, u * MACRO + t * P:u * MACRO + (t + 1) * P, h * 512:(h + 1) * 512],
                                         vo[:, c % 2, :]).then_inc(s["v_st"][c % 2], 16)
                for v in range(U):
                    sp.wait_ge(s["stored"][v], 16)
                if qkv:
                    for v in range(2):
                        sp.wait_ge(s["qk_st"][v], 16 * U * QC // 2)
                        sp.wait_ge(s["g_st"][v], 16 * U * HP // 2)
                        sp.wait_ge(s["v_st"][v], 16 * U * VC // 2)
                end_round(s, sp, b, leader=True)

        @block.tensor
        def _(pe):
            if qkv:
                pe.wait_ge(s["w_in"], 112)
                pe.wait_ge(s["memk"], 1)
                nc.tensor.matmul(ps[3][:, 0:HP * MEM], blocks[:], msq[:], start=True, stop=True).then_inc(s["memk"], 1)
            with pe.Fori(0, B) as b:
                for u in range(U):
                    n = u

                    def turn(k):
                        pe.wait_ge(s["xn"], (n * LNS + k + 1) * TT)
                        for c in range(DC):
                            for t in range(TT):
                                last = nc.tensor.transpose(ps[c][:, t * P:(t + 1) * P],
                                                           xn[:, t, c * P:(c + 1) * P], ident[:])
                        last.then_inc(s["tr"], 1)
                        pe.wait_ge(s["xnT"], (n * LNS + k + 1) * DC)

                    turn(0)
                    for h in range(FC):
                        if h >= 2:
                            pe.wait_ge(s["gelu"], n * FC + h - 1)
                        for c in range(DC):
                            last = nc.tensor.matmul(ps[2 + h % 2][:], Wfc[:, c, h * P:(h + 1) * P], xnT[:, c, :],
                                                    start=(c == 0), stop=(c == DC - 1))
                        last.then_inc(s["hid"], 1)
                    pe.wait_ge(s["gelu"], (n + 1) * FC)
                    pe.wait_ge(s["sq"], (n + 1) * FC)
                    for t in range(TT):
                        for h in range(FC):
                            nc.tensor.matmul(ps[4 + t][:, 0:DIM + 1], gT[:, h, t * P:(t + 1) * P], Wp[:, h, :],
                                             start=(h == 0), stop=(h == FC - 1))
                        for h in range(FC):
                            last = nc.tensor.matmul(ps[4 + t][:, DIM + 1:DIM + 2], g2T[:, h, t * P:(t + 1) * P],
                                                    ones[:, 0:1], start=(h == 0), stop=(h == FC - 1))
                        last.then_inc(s["out"], 1)
                    if not qkv:
                        continue
                    turn(1)
                    for c in range(QC + 1):
                        if c < QC:
                            if c >= 2:
                                pe.wait_ge(s["qk"], n * QC + c - 1)
                            for k in range(DC):
                                last = nc.tensor.matmul(ps[c % 2][:],
                                                        W4[:, c // HP, k, (c % HP) * P:(c % HP + 1) * P],
                                                        xnT[:, k, :], start=(k == 0), stop=(k == DC - 1))
                            last.then_inc(s["proj"], 1)
                        if c >= 1:
                            pe.wait_ge(s["square"], n * QC + c)
                            if c >= 3:
                                pe.wait_ge(s["norm"], n * QC + c - 2)
                            nc.tensor.matmul(ps[2 + (c - 1) % 2][:], blocks[:], sq[:, (c - 1) % 2, :], start=True,
                                             stop=True).then_inc(s["ssq"], 1)
                    for c in range(HP):
                        if c >= 2:
                            pe.wait_ge(s["sig"], n * HP + c - 1)
                        for k in range(DC):
                            last = nc.tensor.matmul(ps[4 + c % 2][:], W4[:, 3, k, c * P:(c + 1) * P], xnT[:, k, :],
                                                    start=(k == 0), stop=(k == DC - 1))
                        last.then_inc(s["gate"], 1)
                    for c in range(VC):
                        t, h = c // 2, c % 2
                        if c >= 2:
                            pe.wait_ge(s["v_out"], n * VC + c - 1)
                        for k in range(DC):
                            last = nc.tensor.matmul(ps[6 + c % 2][:], xnT[:, k, t * P:(t + 1) * P],
                                                    W4[:, 2, k, h * 512:(h + 1) * 512], start=(k == 0),
                                                    stop=(k == DC - 1))
                        last.then_inc(s["val"], 1)
                    pe.wait_ge(s["qk"], (n + 1) * QC)
                end_round(s, pe, b)

        @block.scalar
        def _(act):
            if qkv:
                act.wait_ge(s["w_in"], 112)
                nc.scalar.activation(msq[:], mraw[:], ACT.Square).then_inc(s["memk"], 1)
                act.wait_ge(s["memk"], 2)
                nc.scalar.activation(mrt[:], ps[3][:, 0:HP * MEM], ACT.Sqrt).then_inc(s["memk"], 1)
            with act.Fori(0, B) as b:
                for u in range(U):
                    n = u

                    def norm(k):
                        act.wait_ge(s["stat"], (n * LNS + k + 1))
                        nc.scalar.activation(f["std"][:], f["mv"][:, :, 1], ACT.Sqrt,
                                             bias=eps[:, 0:1]).then_inc(s["std"], 1)
                        act.wait_ge(s["tr"], n * LNS + k + 1)
                        for c in range(DC):
                            nc.scalar.activation(xnT[:, c, :], ps[c][:], ACT.Copy).then_inc(s["xnT"], 1)

                    norm(0)
                    for h in range(FC):
                        act.wait_ge(s["hid"], n * FC + h + 1)
                        nc.scalar.activation(gT[:, h, :], ps[2 + h % 2][:], ACT.Gelu).then_inc(s["gelu"], 1)
                    act.wait_ge(s["hstat"], n + 1)
                    nc.scalar.activation(f["hstd"][:], f["nv"][:], ACT.Sqrt, bias=eps[:, 0:1],
                                         scale=-1.0).then_inc(s["hstd"], 1)
                    if not qkv:
                        continue
                    norm(1)
                    for c in range(QC + 1):
                        if c < QC:
                            act.wait_ge(s["proj"], n * QC + c + 1)
                            if c >= 2:
                                act.wait_ge(s["ssq"], n * QC + c - 1)
                            nc.scalar.activation(sq[:, c % 2, :], ps[c % 2][:], ACT.Square).then_inc(s["square"], 1)
                        if c >= 1:
                            act.wait_ge(s["ssq"], n * QC + c)
                            if c >= 3:
                                act.wait_ge(s["qk"], n * QC + c - 2)
                            nc.scalar.activation(rt[:, (c - 1) % 2, :], ps[2 + (c - 1) % 2][:],
                                                 ACT.Sqrt).then_inc(s["norm"], 1)
                    for c in range(HP):
                        act.wait_ge(s["gate"], n * HP + c + 1)
                        if c >= 2:
                            act.wait_ge(s["gs"], n * HP + c - 1)
                        nc.scalar.activation(sg[:, c % 2, :], ps[4 + c % 2][:], ACT.Sigmoid,
                                             bias=bg[:, c:c + 1]).then_inc(s["sig"], 1)
                end_round(s, act, b)

        @block.gpsimd
        def _(pool):
            with pool.Fori(0, B) as b:
                for u in range(U):
                    n = u
                    for h in range(FC):
                        pool.wait_ge(s["gelu"], n * FC + h + 1)
                        nc.gpsimd.tensor_tensor(g2T[:, h, :], gT[:, h, :], gT[:, h, :], ALU.mult).then_inc(s["sq"], 1)
                    if not qkv:
                        continue
                    for c in range(HP):
                        pool.wait_ge(s["sig"], n * HP + c + 1)
                        if c >= 2:
                            pool.wait_ge(s["g_st"][c % 2], 16 * (n * (HP // 2) + c // 2))
                        nc.gpsimd.tensor_scalar(gs[:, c % 2, :], sg[:, c % 2, :], hs[:, c:c + 1], None,
                                                ALU.mult).then_inc(s["gs"], 1)
                    pool.wait_ge(s["g_st"][0], 16 * (n + 1) * (HP // 2))
                    pool.wait_ge(s["g_st"][1], 16 * (n + 1) * (HP // 2))
                end_round(s, pool, b)

        @block.vector
        def _(dve):

            count = [0]

            def link(ins):
                count[0] += 1
                ins.then_inc(s["link"], 1)
                dve.wait_ge(s["link"], count[0])

            if qkv:
                dve.wait_ge(s["memk"], 3)
                nc.vector.tensor_scalar(mrt[:], mrt[:], L2_EPS, None, ALU.max).then_inc(s["mem"], 1)
                dve.wait_ge(s["mem"], 1)
                nc.vector.reciprocal(msq[:], mrt[:]).then_inc(s["mem"], 1)
                dve.wait_ge(s["mem"], 2)
                nc.vector.tensor_tensor(mkT[:], mraw[:], msq[:], ALU.mult)
            with dve.Fori(0, B) as b:
                for u in range(U):
                    n = u

                    def norm(k):
                        for t in range(TT):
                            link(nc.vector.bn_stats(f["bn"][:, t, :], X[:, u, t, :]))
                            link(nc.vector.bn_aggr(f["mv"][:, t, :], f["bn"][:, t, :]))
                        dve.sem_inc(s["stat"], 1)
                        dve.wait_ge(s["std"], n * LNS + k + 1)
                        link(nc.vector.reciprocal(f["rstd"][:], f["std"][:]))
                        for t in range(TT):
                            nc.vector.tensor_scalar(xn[:, t, :], X[:, u, t, :], f["mv"][:, t, 0:1],
                                                    f["rstd"][:, t:t + 1], ALU.subtract, ALU.mult).then_inc(s["xn"], 1)

                    dve.wait_ge(s["x_in"][u], 16)
                    norm(0)
                    for t in range(TT):
                        dve.wait_ge(s["out"], n * TT + t + 1)
                        link(nc.vector.tensor_scalar(f["st"][:, t, :], ps[4 + t][:, DIM:DIM + 2], 1.0 / HID, None,
                                                     ALU.mult))
                    link(nc.vector.tensor_scalar(f["nmu"][:], f["st"][:, :, 0], -1.0, None, ALU.mult))
                    link(nc.vector.tensor_tensor(f["nv"][:], f["st"][:, :, 0], f["st"][:, :, 0], ALU.mult))
                    nc.vector.tensor_tensor(f["nv"][:], f["nv"][:], f["st"][:, :, 1],
                                            ALU.subtract).then_inc(s["hstat"], 1)
                    dve.wait_ge(s["hstd"], n + 1)
                    link(nc.vector.reciprocal(f["hrstd"][:], f["hstd"][:]))
                    for t in range(TT):
                        link(nc.vector.scalar_tensor_tensor(out=f["t1"][:, t], in0=Bsum[:], scalar=f["nmu"][:, t:t + 1],
                                                            in1=ps[4 + t][:, 0:DIM], op0=ALU.mult, op1=ALU.add))
                        link(nc.vector.scalar_tensor_tensor(out=f["t2"][:, t], in0=f["t1"][:, t],
                                                            scalar=f["hrstd"][:, t:t + 1], in1=Csum[:],
                                                            op0=ALU.mult, op1=ALU.add))
                        nc.vector.scalar_tensor_tensor(out=X[:, u, t], in0=f["t2"][:, t], scalar=0.5,
                                                       in1=X[:, u, t], op0=ALU.mult, op1=ALU.add).then_inc(s["res"], 1)
                    dve.wait_ge(s["res"], (n + 1) * TT)
                    if qkv:
                        norm(1)
                        for c in range(QC):
                            dve.wait_ge(s["norm"], n * QC + c + 1)
                            link(nc.vector.tensor_scalar(rr[:, c % 2, :], rt[:, c % 2, :], L2_EPS, None, ALU.max))
                            link(nc.vector.reciprocal(ri[:, c % 2, :], rr[:, c % 2, :]))
                            if c >= 2:
                                dve.wait_ge(s["qk_st"][c % 2], 16 * (n * (QC // 2) + c // 2))
                            nc.vector.scalar_tensor_tensor(out=qn[:, c % 2, :], in0=ps[c % 2][:],
                                                           scalar=QK_SCALE if c < HP else 1.0, in1=ri[:, c % 2, :],
                                                           op0=ALU.mult, op1=ALU.mult).then_inc(s["qk"], 1)
                        dve.wait_ge(s["qk_st"][0], 16 * (n + 1) * (QC // 2))
                        dve.wait_ge(s["qk_st"][1], 16 * (n + 1) * (QC // 2))
                        for c in range(VC):
                            dve.wait_ge(s["val"], n * VC + c + 1)
                            if c >= 2:
                                dve.wait_ge(s["v_st"][c % 2], 16 * (n * (VC // 2) + c // 2))
                            nc.vector.tensor_copy(vo[:, c % 2, :], ps[6 + c % 2][:]).then_inc(s["v_out"], 1)
                        dve.wait_ge(s["v_st"][0], 16 * (n + 1) * (VC // 2))
                        dve.wait_ge(s["v_st"][1], 16 * (n + 1) * (VC // 2))
                end_round(s, dve, b)


def attention(nc, ps, mkT, qd, kd, gd, vd, x1d, x2d, sd, pre_th, post_th, mem_v, Wo_d, delta_c, mask_c):
    S = IB * TPB
    MPC = [len(pieces(width(s // TPB))) for s in range(S)]
    MCUM = [sum(MPC[:s]) for s in range(S + 1)]
    HPC = [len(pieces(width(k // H))) for k in range(IB * H)]
    HCUM = [sum(HPC[:k]) for k in range(IB * H + 1)]
    PG = [-(-(s // TPB + 1) // 4) + 1 for s in range(S)]
    PCUM = [sum(PG[:s]) for s in range(S + 1)]
    LT = 2 * (TOPK // 8)
    SNR = 2
    SLOT = [k % SNR for k in range(IB * H)]
    STORES = [[sum(1 for j in range(k) if SLOT[j] == v) for k in range(IB * H + 1)] for v in range(SNR)]
    SPB = [STORES[v][-1] for v in range(SNR)]
    RSLOT = [i % DRING for i in range(S)]
    LOADS = [[sum(1 for j in range(i) if RSLOT[j] == v) for i in range(S + 1)] for v in range(DRING)]

    with ExitStack() as ctx:
        def sb(name, shape):
            return ctx.enter_context(nc.sbuf_tensor(name, shape, F32))
        kT = sb("kT", [P, HP, JW])
        V = sb("V", [P, IB, INNER])
        vm = sb("vm", [MEM, INNER])
        qT = sb("qT", [P, 2, HP, P])
        gT = sb("gateT", [P, 2, HP, P])
        Sn = sb("Sn", [P, SNR, JW])
        Sg = sb("Sg", [P, DRING, JW])
        D = sb("D", [P, DRING, JW])
        W = sb("W", [P, JW])
        E = sb("E", [P, 2, JW])
        AT = sb("AT", [P, IB, H, P // 2])
        ATm = sb("ATm", [MEM, H, P // 2])
        UT = sb("UT", [P, HP, P])
        Wo = sb("Wo", [P, HP, DIM])
        x1 = sb("x1", [P, 2, DIM])
        x2 = sb("x2", [P, 2, DIM])
        delta = sb("delta", [P, P])
        wrep = sb("wrep", [P, 2, H])
        kpre = sb("kpre", [P, H, R8])
        kpost = sb("kpost", [P, H, R8])
        kr = sb("kr", [P, 2, H * R8])
        mask = sb("mask", [P, 2 * P - R8])
        top8 = sb("top8", [P, 2, TOPK])
        nmax = sb("nmax", [P, 2])
        rs = sb("rs", [P, 2])
        ri = sb("rinv", [P, 2])
        s = semaphores(nc, ctx, "t", dict(c_in=1, kpre=1, k_in=IB, v_in=IB, q_in=2, g_in=2, mem_k=1, s_ps=1, s_sb=1,
                                    s_st=SNR, sg_in=DRING, mixed=1, d_raw=1, d_ok=1, topk=1, nm=1, exp=1,
                                    rinv=1, kr=1, post=1, at=1, av=1, ut=1, y=1, x_in=2, x_ok=1,
                                    x_st=2), keep=("c_in", "kpre"))
        block = ctx.enter_context(nc.Block())

        @block.sync
        def _(sp):
            sp.dma_start(delta[:], delta_c).then_inc(s["c_in"], 16)
            sp.dma_start(mask[:], mask_c).then_inc(s["c_in"], 16)
            sp.dma_start(Wo[:], Wo_d.rearrange("(c p) n -> p c n", p=P)).then_inc(s["c_in"], 16)
            sp.dma_start(vm[:], mem_v).then_inc(s["c_in"], 16)
            for i, th in enumerate((pre_th, post_th)):
                for g in range(H):
                    sp.dma_start(wrep[g * R8:(g + 1) * R8, i, :],
                                 th[g:g + 1, :].broadcast_to([R8, H])).then_inc(s["c_in"], 16)
            with sp.Fori(0, B) as b:
                def keys(ib):
                    r = slice(ib * P, (ib + 1) * P)
                    sp.dma_start(kT[:, :, MEM + ib * P:MEM + (ib + 1) * P], kd[b, :, :, r]).then_inc(s["k_in"][ib], 16)
                    if ib >= 2:
                        sp.wait_ge(s["s_ps"], HCUM[H * (ib - 1)])
                    sp.dma_start(qT[:, ib % 2], qd[b, :, :, r]).then_inc(s["q_in"][ib % 2], 16)

                def late(ib):
                    r = slice(ib * P, (ib + 1) * P)
                    sp.dma_start(V[:, ib, :], vd[b, r, :]).then_inc(s["v_in"][ib], 16)
                    if ib >= 2:
                        sp.wait_ge(s["ut"], 2 * (ib - 1))
                    sp.dma_start(gT[:, ib % 2], gd[b, :, :, r]).then_inc(s["g_in"][ib % 2], 16)
                    if ib >= 2:
                        sp.wait_ge(s["x_ok"], ib - 1)
                    sp.dma_start(x1[:, ib % 2], x1d[b, r, :]).then_inc(s["x_in"][ib % 2], 16)

                def store(ib, h):
                    k = ib * H + h
                    n = width(ib)
                    sp.wait_ge(s["s_sb"], HCUM[k + 1])
                    sp.dma_start(sd[ib % 2, h, :, 0:n], Sn[:, SLOT[k], 0:n]).then_inc(s["s_st"][SLOT[k]], 16)

                def load(i):
                    ib, t = i // TPB, i % TPB
                    n = width(ib)
                    if t == 0:
                        for v in range(SNR):
                            sp.wait_ge(s["s_st"][v], 16 * (STORES[v][H * (ib + 1)]))
                    if i >= DRING:
                        sp.wait_ge(s["mixed"], MCUM[i - DRING + 1])
                    sp.dma_start(Sg[:, RSLOT[i], 0:n],
                                 sd[ib % 2, :, t * R8:(t + 1) * R8, 0:n]).then_inc(s["sg_in"][RSLOT[i]], 16)

                keys(0)
                for h in range(H):
                    store(0, h)
                keys(1)
                late(0)
                for i in range(DRING):
                    load(i)
                for i in range(S):
                    ib, t = i // TPB, i % TPB
                    if t < H // 2 and ib + 1 < IB:
                        store(ib + 1, 2 * t)
                        store(ib + 1, 2 * t + 1)
                    if i + DRING < S:
                        load(i + DRING)
                    if t == 10 and ib >= 1:
                        sp.wait_ge(s["x_ok"], ib)
                        sp.dma_start(x2d[b, (ib - 1) * P:ib * P, :],
                                     x2[:, (ib - 1) % 2]).then_inc(s["x_st"][(ib - 1) % 2], 16)
                    if t == 8 and ib + 2 < IB:
                        keys(ib + 2)
                    if t == 12 and ib + 1 < IB:
                        late(ib + 1)
                sp.wait_ge(s["x_ok"], IB)
                sp.dma_start(x2d[b, (IB - 1) * P:IB * P, :],
                             x2[:, (IB - 1) % 2]).then_inc(s["x_st"][(IB - 1) % 2], 16)
                for v in range(2):
                    sp.wait_ge(s["x_st"][v], 16 * IB // 2)
                end_round(s, sp, b, leader=True)

        @block.tensor
        def _(pe):
            pe.wait_ge(s["c_in"], 16 * (4 + 2 * H))
            pe.wait_ge(s["kpre"], 2)
            with pe.Fori(0, B) as b:
                def scores(ib, h):
                    k = ib * H + h
                    if h == 0:
                        pe.wait_ge(s["k_in"][ib], 16)
                        if ib == 0:
                            pe.wait_ge(s["mem_k"], 1)
                        pe.wait_ge(s["q_in"][ib % 2], 16 * (ib // 2 + 1))
                    lo = DH * (h % 2)
                    for i, (c0, c1) in enumerate(pieces(width(ib))):
                        m = HCUM[k] + i
                        if m >= 2:
                            pe.wait_ge(s["s_sb"], m - 1)
                        nc.tensor.matmul(ps[m % 2][:, 0:c1 - c0], qT[lo:lo + DH, ib % 2, h // 2, :],
                                         kT[lo:lo + DH, h // 2, c0:c1], start=True, stop=True).then_inc(s["s_ps"], 1)

                def mix(i):
                    pe.wait_ge(s["sg_in"][RSLOT[i]], 16 * (LOADS[RSLOT[i]][i + 1]))
                    for k, (c0, c1) in enumerate(pieces(width(i // TPB))):
                        m = MCUM[i] + k
                        if m >= 2:
                            pe.wait_ge(s["d_raw"], m - 1)
                        nc.tensor.matmul(ps[2 + m % 2][:, 0:c1 - c0], kpre[:].rearrange("p h r -> p (h r)"),
                                         Sg[:, RSLOT[i], c0:c1], start=True, stop=True).then_inc(s["mixed"], 1)

                def post(i):
                    ib = i // TPB
                    pe.wait_ge(s["topk"], (i + 1) * LT)
                    pe.wait_ge(s["kr"], i + 1)
                    for g in range(PG[i]):
                        m = PCUM[i] + g
                        if m >= 2:
                            pe.wait_ge(s["at"], m - 1)
                        bank = ps[4 + m % 2]
                        if g == 0:
                            last = nc.tensor.matmul(bank[0:MEM, 0:P], E[:, i % 2, 0:MEM], kr[:, i % 2, :],
                                                    start=True, stop=True)
                        else:
                            for c in range(4 * (g - 1), min(4 * g, ib + 1)):
                                last = nc.tensor.matmul(bank[:, (c % 4) * P:(c % 4 + 1) * P],
                                                        E[:, i % 2, MEM + c * P:MEM + (c + 1) * P],
                                                        kr[:, i % 2, :], start=True, stop=True)
                        last.then_inc(s["post"], 1)

                def values(hb):
                    ib = hb // 2
                    pe.wait_ge(s["at"], PCUM[(hb + 1) * TPH])
                    if hb % 2 == 0:
                        pe.wait_ge(s["v_in"][ib], 16)
                    if hb >= 1:
                        pe.wait_ge(s["ut"], hb)
                    for h in range(H):
                        lo = DH * (h % 2)
                        dst = ps[6][lo:lo + DH, (h // 2) * DH:(h // 2 + 1) * DH]
                        for c in range(ib + 1):
                            nc.tensor.matmul(dst, V[:, c, h * DH:(h + 1) * DH], AT[:, c, h, :], start=(c == 0),
                                             stop=False)
                        last = nc.tensor.matmul(dst, vm[:, h * DH:(h + 1) * DH], ATm[:, h, :], start=False, stop=True)
                    last.then_inc(s["av"], 1)

                def project(ib):
                    pe.wait_ge(s["ut"], 2 * (ib + 1))
                    if ib >= 1:
                        pe.wait_ge(s["x_ok"], ib)
                    for p in range(HP):
                        last = nc.tensor.matmul(ps[7][:, 0:DIM], UT[:, p, :], Wo[:, p, :], start=(p == 0),
                                                stop=(p == HP - 1))
                    last.then_inc(s["y"], 1)

                def tail(i):
                    post(i)
                    if i % TPH == TPH - 1:
                        values(i // TPH)

                for h in range(H):
                    scores(0, h)
                for i in range(S):
                    ib, t = i // TPB, i % TPB
                    mix(i)
                    if t < H // 2 and ib + 1 < IB:
                        scores(ib + 1, 2 * t)
                        scores(ib + 1, 2 * t + 1)
                    if i >= 2:
                        tail(i - 2)
                    if t == 5 and ib >= 1:
                        project(ib - 1)
                tail(S - 2)
                tail(S - 1)
                project(IB - 1)
                pe.wait_ge(s["x_ok"], IB)
                end_round(s, pe, b)

        @block.scalar
        def _(act):
            with act.Fori(0, B) as b:
                def scores(ib, h):
                    k = ib * H + h
                    if k >= SNR:
                        act.wait_ge(s["s_st"][SLOT[k]], 16 * (STORES[SLOT[k]][k]))
                    for i, (c0, c1) in enumerate(pieces(width(ib))):
                        m = HCUM[k] + i
                        act.wait_ge(s["s_ps"], m + 1)
                        nc.scalar.activation(Sn[:, SLOT[k], c0:c1], ps[m % 2][:, 0:c1 - c0],
                                             ACT.Copy).then_inc(s["s_sb"], 1)

                def mixed(i):
                    if i >= DRING:
                        act.wait_ge(s["topk"], (i - DRING + 1) * LT)
                    for k, (c0, c1) in enumerate(pieces(width(i // TPB))):
                        m = MCUM[i] + k
                        act.wait_ge(s["mixed"], m + 1)
                        nc.scalar.activation(D[:, RSLOT[i], c0:c1], ps[2 + m % 2][:, 0:c1 - c0],
                                             ACT.Copy).then_inc(s["d_raw"], 1)

                def exps(i):
                    n = width(i // TPB)
                    act.wait_ge(s["topk"], i * LT + 1)
                    nc.scalar.mul(nmax[:, i % 2:i % 2 + 1], top8[:, i % 2, 0:1], -1.0).then_inc(s["nm"], 1)
                    act.wait_ge(s["nm"], i + 1)
                    act.wait_ge(s["d_ok"], i + 1)
                    if i >= 2:
                        act.wait_ge(s["post"], PCUM[i - 1])
                    nc.scalar.activation(E[:, i % 2, 0:n], D[:, RSLOT[i], 0:n], ACT.Exp,
                                         bias=nmax[:, i % 2:i % 2 + 1]).then_inc(s["exp"], 1)

                def turned(i):
                    ib, t = i // TPB, i % TPH
                    if t == 0 and i >= TPH:
                        act.wait_ge(s["av"], i // TPH)
                    for g in range(PG[i]):
                        m = PCUM[i] + g
                        act.wait_ge(s["post"], m + 1)
                        bank = ps[4 + m % 2]
                        if g == 0:
                            dst = ATm[:, :, t * R8:(t + 1) * R8]
                            src = bank[0:MEM, 0:P].rearrange("p (h r) -> p h r", h=H)
                        else:
                            c0, c1 = 4 * (g - 1), min(4 * g, ib + 1)
                            dst = AT[:, c0:c1, :, t * R8:(t + 1) * R8]
                            src = bank[:, 0:(c1 - c0) * P].rearrange("p (c h r) -> p c h r", h=H, r=R8)
                        nc.scalar.activation(dst, src, ACT.Copy).then_inc(s["at"], 1)

                for h in range(H):
                    scores(0, h)
                for i in range(S):
                    ib, t = i // TPB, i % TPB
                    mixed(i)
                    if t < H // 2 and ib + 1 < IB:
                        scores(ib + 1, 2 * t)
                        scores(ib + 1, 2 * t + 1)
                    if i >= 2:
                        exps(i - 2)
                        turned(i - 2)
                for i in (S - 2, S - 1):
                    exps(i)
                    turned(i)
                end_round(s, act, b)

        @block.gpsimd
        def _(pool):
            pool.wait_ge(s["c_in"], 16 * (4 + 2 * H))
            for i, k in enumerate((kpre, kpost)):
                for h in range(H):
                    last = nc.gpsimd.tensor_scalar(k[:, h, :], delta[:, 0:R8], wrep[:, i, h:h + 1], None, ALU.mult)
                last.then_inc(s["kpre"], 1)
            pool.wait_ge(s["kpre"], 2)
            pool.wait_ge(s["c_in"], 16 * (4 + 2 * H))
            with pool.Fori(0, B) as b:
                nc.gpsimd.tensor_copy(kT[:, :, 0:MEM], mkT[:].rearrange("p (c m) -> p c m", c=HP)).then_inc(s["mem_k"], 1)

                def causal(i):
                    ib, t = i // TPB, i % TPB
                    n = width(ib)
                    pool.wait_ge(s["d_raw"], MCUM[i + 1])
                    d = D[:, RSLOT[i], n - P:n]
                    nc.gpsimd.tensor_tensor(d, d, mask[:, P - R8 - R8 * t:2 * P - R8 - R8 * t],
                                            ALU.add).then_inc(s["d_ok"], 1)

                def spread(i):
                    pool.wait_ge(s["rinv"], i + 1)
                    if i >= 2:
                        pool.wait_ge(s["post"], PCUM[i - 1])
                    nc.gpsimd.tensor_scalar(kr[:, i % 2, :], kpost[:].rearrange("p h r -> p (h r)"),
                                            ri[:, i % 2:i % 2 + 1], None, ALU.mult).then_inc(s["kr"], 1)

                for i in range(S):
                    causal(i)
                    if i >= 2:
                        spread(i - 2)
                spread(S - 2)
                spread(S - 1)
                end_round(s, pool, b)

        @block.vector
        def _(dve):
            with dve.Fori(0, B) as b:
                def topk(i):
                    n = width(i // TPB)
                    d, w, e = D[:, RSLOT[i], 0:n], W[:, 0:n], E[:, i % 2, 0:n]
                    count = [0]

                    def link(ins):
                        count[0] += 1
                        ins.then_inc(s["topk"], 1)
                        dve.wait_ge(s["topk"], i * LT + count[0])

                    dve.wait_ge(s["d_ok"], i + 1)
                    if i >= 2:
                        dve.wait_ge(s["exp"], i - 1)
                    for r in range(TOPK // 8):
                        t8 = top8[:, i % 2, 8 * r:8 * r + 8]
                        ins = nc.vector.max(t8, d if r == 0 else w)
                        link(ins)
                        if r < TOPK // 8 - 1:
                            link(nc.vector.match_replace(out=w, in_to_replace=t8, in_values=d if r == 0 else w,
                                                         imm_value=NEG))
                    dve.wait_ge(s["exp"], i + 1)
                    link(nc.vector.scalar_tensor_tensor(out=e, in0=d, scalar=top8[:, i % 2, TOPK - 1:TOPK], in1=e,
                                                        op0=ALU.is_ge, op1=ALU.mult,
                                                        accum_out=rs[:, i % 2:i % 2 + 1]))
                    if i >= 2:
                        dve.wait_ge(s["kr"], i - 1)
                    nc.vector.reciprocal(ri[:, i % 2:i % 2 + 1], rs[:, i % 2:i % 2 + 1]).then_inc(s["rinv"], 1)
                    assert count[0] == LT

                def gated(hb):
                    ib = hb // 2
                    dve.wait_ge(s["av"], hb + 1)
                    if hb % 2 == 0:
                        dve.wait_ge(s["g_in"][ib % 2], 16 * (ib // 2 + 1))
                        if ib >= 1:
                            dve.wait_ge(s["y"], ib)
                    o = (hb % 2) * (P // 2)
                    nc.vector.tensor_tensor(UT[:, :, o:o + P // 2], ps[6][:].rearrange("p (c r) -> p c r", c=HP),
                                            gT[:, ib % 2, :, o:o + P // 2], ALU.mult).then_inc(s["ut"], 1)

                def residual(ib):
                    dve.wait_ge(s["y"], ib + 1)
                    dve.wait_ge(s["x_in"][ib % 2], 16 * (ib // 2 + 1))
                    if ib >= 2:
                        dve.wait_ge(s["x_st"][ib % 2], 16 * (ib // 2))
                    nc.vector.tensor_tensor(x2[:, ib % 2, :], ps[7][:, 0:DIM], x1[:, ib % 2, :],
                                            ALU.add).then_inc(s["x_ok"], 1)

                for i in range(S):
                    topk(i)
                    if i % TPH == 2 and i >= TPH:
                        gated(i // TPH - 1)
                    if i % TPB == 6 and i >= TPB:
                        residual(i // TPB - 1)
                gated(2 * IB - 1)
                residual(IB - 1)
                end_round(s, dve, b)


def kernel(L0_attn_x, L0_attn_Wq, L0_attn_Wk, L0_attn_Wv, L0_attn_W_pre_th, L0_attn_W_post_th, L0_attn_mem_k,
           L0_attn_mem_v, L0_attn_head_scale_params, L0_attn_Wg, L0_attn_bg, L0_attn_Wo, L0_ffn_W_fc, L0_ffn_ln_w,
           L0_ffn_ln_b, L0_ffn_W_proj):
    import concourse.bacc as bacc
    from concourse.bass_utils import run_bass_kernel_spmd

    nc = bacc.Bacc("TRN2", target_bir_lowering=False, num_devices=1)
    pair_cols = lambda v: np.asarray(v).reshape(HP, P).T
    head = np.asarray(L0_attn_head_scale_params).reshape(H, 1)
    p = np.arange(P)
    u = np.arange(2 * P - R8)
    layout = dict(
        x=np.asarray(L0_attn_x),
        Wq=np.asarray(L0_attn_Wq), Wk=np.asarray(L0_attn_Wk), Wv=np.asarray(L0_attn_Wv),
        pre_th=np.asarray(L0_attn_W_pre_th).T, post_th=np.asarray(L0_attn_W_post_th).T,
        mem_kT=np.asarray(L0_attn_mem_k).reshape(HP, 2, MEM, DH).transpose(1, 3, 0, 2).reshape(P, HP * MEM),
        mem_v=np.asarray(L0_attn_mem_v).transpose(1, 0, 2).reshape(MEM, INNER),
        hs_col=pair_cols(np.broadcast_to(head, (H, DH)).reshape(-1)),
        Wg=np.asarray(L0_attn_Wg), bg_col=pair_cols(L0_attn_bg), Wo=np.asarray(L0_attn_Wo),
        WfcT=np.asarray(L0_ffn_W_fc).T,
        lnw_col=np.asarray(L0_ffn_ln_w).reshape(FC, P).T, lnb_col=np.asarray(L0_ffn_ln_b).reshape(FC, P).T,
        WpT=np.asarray(L0_ffn_W_proj).T,
        ident_c=np.eye(P, dtype=np.float32),
        blocks_c=(p[:, None] // DH == p[None, :] // DH).astype(np.float32),
        delta_c=(p[:, None] % R8 == p[None, :] % R8).astype(np.float32),
        mask_c=np.where(u[None, :] - (P - R8) <= p[:, None] % R8, np.float32(0), np.float32(NEG)),
    )
    arrays, args = {}, []
    for name, a in layout.items():
        a = np.ascontiguousarray(a)
        arrays[f"in_{name}"] = a
        args.append(nc.dram_tensor(f"in_{name}", a.shape, mybir.dt.from_np(a.dtype), kind="ExternalInput").ap())
    out = nc.dram_tensor("out_x", (B, N, DIM), F32, kind="ExternalOutput").ap()
    build(nc, *args, out)
    r = run_bass_kernel_spmd(nc, [arrays], core_ids=[0])
    return r.results[0]["out_x"]
```

```python
import math
import numpy as np
import concourse.bass as bass
import concourse.mybir as mybir
from contextlib import ExitStack

B, N, DIM = 4, 1024, 256
H, DH = 16, 64
MEM, TOPK = 4, 64
HID = 1024
P = 128
DC = DIM // P
FC = HID // P
HP = H // 2
INNER = H * DH
MACRO = 512
U = N // MACRO
TT = MACRO // P
IB = N // P
R8 = P // H
TPB = P // R8
TPH = TPB // 2
JW = MEM + N
FFN_W = DC * HID + FC * (DIM + 1) + 2 * DIM
LN_EPS = 1e-5
Q_EPS = 1e-6
L2_EPS = 1e-12
QK_SCALE = 10.0
NEG = float(np.finfo(np.float32).min)
MASKED = -2.0 ** 40
DRING = 2
RING = 6
FAST_IB = 1
DAMP = (0.95, 0.65)
SMALL = 2.0 ** -50
F32 = mybir.dt.float32
ALU = mybir.AluOpType
ACT = mybir.ActivationFunctionType


def width(ib):
    return MEM + P * (ib + 1)


def pieces(n):
    k = -(-n // 512)
    cuts = [n * i // k for i in range(k + 1)]
    return list(zip(cuts[:-1], cuts[1:]))


def semaphores(nc, ctx, prefix, names, keep=()):
    made = {name: [ctx.enter_context(nc.semaphore(f"{prefix}_{name}{i}")) for i in range(count)]
            for name, count in names.items()}
    rounds = [sem for name, sems in made.items() if name not in keep for sem in sems]
    ends = {name: ctx.enter_context(nc.semaphore(f"{prefix}_{name}")) for name in ("arrive", "go", "passed")}
    return {"rounds": rounds, **ends, **{name: sems if len(sems) > 1 else sems[0] for name, sems in made.items()}}


def end_round(s, eng, b, leader=False):
    eng.drain().then_inc(s["arrive"], 1)
    if leader:
        eng.wait_ge(s["arrive"], 5 * (b + 1))
        eng.sem_inc(s["passed"], 1)
        for sem in s["rounds"]:
            eng.sem_clear(sem)
        eng.sem_inc(s["go"], 1)
    eng.wait_ge(s["go"], b + 1)
    eng.sem_inc(s["passed"], 1)


def ffn_buffers(nc, ctx, tag):
    def sb(name, shape):
        return ctx.enter_context(nc.sbuf_tensor(f"{tag}_{name}", shape, F32))
    b = {}
    b["x"] = sb("x", [P, 2, TT, DIM])
    b["xn"] = sb("xn", [P, TT, DIM])
    b["xnT"] = sb("xnT", [P, DC, MACRO])
    b["gT"] = sb("gT", [P, FC, MACRO])
    b["g2T"] = sb("g2T", [P, FC, MACRO])
    b["bn"] = sb("bn", [P, TT, 6])
    b["mv"] = sb("mv", [P, TT, 2])
    b["std"] = sb("std", [P, TT])
    b["rstd"] = sb("rstd", [P, TT])
    b["st"] = sb("st", [P, TT, 2])
    b["nv"] = sb("nv", [P, TT])
    b["nmu"] = sb("nmu", [P, TT])
    b["hstd"] = sb("hstd", [P, TT])
    b["hrstd"] = sb("hrstd", [P, TT])
    b["t1"] = sb("t1", [P, TT, DIM])
    b["t2"] = sb("t2", [P, TT, DIM])
    return b


FFN_SEMS = dict(gsum=1, x_in=2, stat=1, std=1, xn=1, tr=1, xnT=1, hid=1, gelu=1, sq=1,
                out=1, hstat=1, hstd=1, res=1, stored=2, link=1)
QKV_SEMS = dict(proj=1, square=1, ssq=1, norm=1, qk=1, qk_st=2, gate=1, sig=1, gs=1, g_st=2, val=1, v_out=1,
                v_st=2)


def build(nc, x, Wq, Wk, Wv, pre_th, post_th, mem_kT, mem_v, hs_col, Wg, bg_col, Wo, WfcT, lnw_col, lnb_col, WpT,
          ident_c, blocks_c, delta_c, mask_c, guess_c, out):
    def dram(name, shape):
        return nc.dram_tensor(name, shape, F32, kind="Internal").ap()
    qd = dram("q_scratch", [B, P, HP, N])
    kd = dram("k_scratch", [B, P, HP, N])
    gd = dram("gate_scratch", [B, P, HP, N])
    vd = dram("v_scratch", [B, N, INNER])
    x1d = dram("x1_scratch", [B, N, DIM])
    x2d = dram("x2_scratch", [B, N, DIM])
    sd = dram("score_scratch", [2, H, P, JW])
    wd = dram("weight_scratch", [P, FFN_W])

    with ExitStack() as top:
        def sb(name, shape):
            return top.enter_context(nc.sbuf_tensor(name, shape, F32))
        ps = [top.enter_context(nc.psum_tensor(f"bank{i}", [P, 512], F32)) for i in range(8)]
        ident = sb("ident", [P, P])
        ones = sb("ones", [P, P])
        eps = sb("eps", [P, 1])
        mkT = sb("mkT", [P, HP * MEM])
        with ExitStack() as ctx:
            ffn_w = ctx.enter_context(nc.sbuf_tensor("ffn_w1", [P, FFN_W], F32))
            blocks = ctx.enter_context(nc.sbuf_tensor("blocks", [P, P], F32))
            weights_setup(nc, ps, ident, blocks, ones, ffn_w, wd, eps, ident_c, blocks_c, WfcT, WpT, lnw_col, lnb_col)
            token_stage(nc, (ps, ident, ones, ffn_w, eps), "a", x, x1d,
                        qkv=(blocks, Wq, Wk, Wv, Wg, bg_col, hs_col, mem_kT, mkT, qd, kd, vd, gd))
        attention(nc, ps, mkT, ones, qd, kd, gd, vd, x1d, x2d, sd, pre_th, post_th, mem_v, Wo, delta_c, mask_c,
                  guess_c)
        with ExitStack() as ctx:
            ffn_w = ctx.enter_context(nc.sbuf_tensor("ffn_w2", [P, FFN_W], F32))
            token_stage(nc, (ps, ident, ones, ffn_w, eps), "c", x2d, out, wd=wd)


def ffn_views(ffn_w):
    a = DC * HID
    b = a + FC * (DIM + 1)
    return (ffn_w[:, 0:a].rearrange("p (c f) -> p c f", c=DC), ffn_w[:, a:b].rearrange("p (c f) -> p c f", c=FC),
            ffn_w[:, b:b + DIM], ffn_w[:, b + DIM:b + 2 * DIM])


def weights_setup(nc, ps, ident, blocks, ones, ffn_w, wd, eps, ident_c, blocks_c, WfcT, WpT, lnw_col, lnb_col):
    Wfc, Wp, Bsum, Csum = ffn_views(ffn_w)
    with ExitStack() as ctx:
        def sb(name, shape):
            return ctx.enter_context(nc.sbuf_tensor(name, shape, F32))
        raw = sb("w_raw", [P, 2, HID * DC])
        absw = sb("w_abs", [P, 2, HID * DC])
        asum = sb("w_asum", [P, 2])
        thr = sb("w_thr", [P, 2])
        nthr = sb("w_nthr", [P, 2])
        neg = sb("w_neg", [P, 2, HID * DC])
        tern = sb("w_tern", [P, HID * DC])
        wb = sb("w_b", [P, FC, DIM])
        lnw = sb("lnw", [P, FC])
        lnb = sb("lnb", [P, FC])
        s = semaphores(nc, ctx, "w", dict(load=1, asum=1, ones=1, tot=1, link=1, wp=1, sums=1, done=1, kept=1))
        block = ctx.enter_context(nc.Block())

        @block.sync
        def _(sp):
            sp.dma_start(raw[:, 0, :].rearrange("p (c f) -> p c f", c=DC),
                         WfcT.rearrange("(c p) f -> p c f", p=P)).then_inc(s["load"], 16)
            sp.dma_start(raw[:, 1, :].rearrange("p (c f) -> p c f", c=FC),
                         WpT.rearrange("(c p) f -> p c f", p=P)).then_inc(s["load"], 16)
            sp.dma_start(lnw[:], lnw_col).then_inc(s["load"], 16)
            sp.dma_start(lnb[:], lnb_col).then_inc(s["load"], 16)
            sp.dma_start(ident[:], ident_c).then_inc(s["load"], 16)
            sp.dma_start(blocks[:], blocks_c).then_inc(s["load"], 16)
            sp.wait_ge(s["done"], 2)
            sp.dma_start(wd, ffn_w[:]).then_inc(s["kept"], 16)
            sp.wait_ge(s["kept"], 16)

        @block.scalar
        def _(act):
            act.wait_ge(s["load"], 96)
            for i in range(2):
                nc.scalar.activation(absw[:, i, :], raw[:, i, :], ACT.Abs,
                                     accum_out=asum[:, i:i + 1]).then_inc(s["asum"], 1)

        @block.tensor
        def _(pe):
            pe.wait_ge(s["ones"], 1)
            pe.wait_ge(s["asum"], 2)
            nc.tensor.matmul(ps[0][:, 0:2], ones[:], asum[:], start=True, stop=True).then_inc(s["tot"], 1)
            pe.wait_ge(s["wp"], 2)
            for c in range(FC):
                nc.tensor.matmul(ps[1][:, 0:DIM], ones[:], Wp[:, c, 0:DIM], start=(c == 0), stop=(c == FC - 1))
            for c in range(FC):
                last = nc.tensor.matmul(ps[2][:, 0:DIM], ones[:], wb[:, c, :], start=(c == 0), stop=(c == FC - 1))
            last.then_inc(s["sums"], 1)

        @block.vector
        def _(dve):
            count = [0]

            def link(ins):
                count[0] += 1
                ins.then_inc(s["link"], 1)
                dve.wait_ge(s["link"], count[0])

            nc.vector.memset(eps[:], LN_EPS)
            nc.vector.memset(Wp[:, :, DIM:DIM + 1], 1.0)
            nc.vector.memset(ones[:], 1.0).then_inc(s["ones"], 1)
            dve.wait_ge(s["load"], 96)
            dve.wait_ge(s["tot"], 1)
            link(nc.vector.tensor_scalar(thr[:], ps[0][:, 0:2], 1.0 / (DIM * HID), Q_EPS, ALU.mult, ALU.add))
            link(nc.vector.tensor_scalar(nthr[:], thr[:], -0.5, None, ALU.mult))
            link(nc.vector.tensor_scalar(thr[:], thr[:], 0.5, None, ALU.mult))
            for i in range(2):
                link(nc.vector.tensor_scalar(neg[:, i, :], raw[:, i, :], nthr[:, i:i + 1], None, ALU.is_lt))
            nc.vector.scalar_tensor_tensor(out=ffn_w[:, 0:DC * HID], in0=raw[:, 0, :],
                                           scalar=thr[:, 0:1], in1=neg[:, 0, :], op0=ALU.is_gt, op1=ALU.subtract)
            link(nc.vector.scalar_tensor_tensor(out=tern[:], in0=raw[:, 1, :], scalar=thr[:, 1:2], in1=neg[:, 1, :],
                                                op0=ALU.is_gt, op1=ALU.subtract))
            for c in range(FC):
                nc.vector.tensor_scalar(wb[:, c, :], tern[:, c * DIM:(c + 1) * DIM], lnb[:, c:c + 1], None, ALU.mult)
                last = nc.vector.tensor_scalar(Wp[:, c, 0:DIM], tern[:, c * DIM:(c + 1) * DIM], lnw[:, c:c + 1], None,
                                               ALU.mult)
            last.then_inc(s["wp"], 2)
            dve.wait_ge(s["sums"], 1)
            nc.vector.tensor_copy(Bsum, ps[1][:, 0:DIM]).then_inc(s["done"], 1)
            nc.vector.tensor_copy(Csum, ps[2][:, 0:DIM]).then_inc(s["done"], 1)


def token_stage(nc, consts, tag, src, dst, qkv=None, wd=None):
    ps, ident, ones, ffn_w, eps = consts
    Wfc, Wp, Bsum, Csum = ffn_views(ffn_w)
    with ExitStack() as ctx:
        def sb(name, shape):
            return ctx.enter_context(nc.sbuf_tensor(name, shape, F32))
        f = ffn_buffers(nc, ctx, tag)
        X, xn, xnT, gT, g2T = f["x"], f["xn"], f["xnT"], f["gT"], f["g2T"]
        LNS = 2 if qkv else 1
        names = dict(FFN_SEMS, ffn_w=1)
        if qkv:
            names.update(QKV_SEMS)
            names.update(dict(w_in=1, memk=1, mem=1))
        s = semaphores(nc, ctx, tag, names, keep=("w_in", "memk", "mem", "ffn_w"))
        if qkv:
            blocks, Wq_d, Wk_d, Wv_d, Wg_d, bg_col, hs_col, mem_kT, mkT, qd, kd, vd, gd = qkv
            W4 = sb("W4", [P, 4, DC, INNER])
            bg = sb("bg", [P, HP])
            hs = sb("hs", [P, HP])
            mraw = sb("mraw", [P, HP * MEM])
            msq = sb("msq", [P, HP * MEM])
            mrt = sb("mrt", [P, HP * MEM])
            sq = sb("sq", [P, 2, MACRO])
            rt = sb("rt", [P, 2, MACRO])
            rr = sb("rr", [P, 2, MACRO])
            ri = sb("ri", [P, 2, MACRO])
            qn = sb("qn", [P, 2, MACRO])
            sg = sb("sg", [P, 2, MACRO])
            gs = sb("gs", [P, 2, MACRO])
            vo = sb("vo", [P, 2, MACRO])
        QC = 2 * HP
        VC = TT * (INNER // 512)
        QB = (0, 1, 4, 5)
        block = ctx.enter_context(nc.Block())

        @block.sync
        def _(sp):
            if not qkv:
                sp.dma_start(ffn_w[:], wd).then_inc(s["ffn_w"], 16)
            if qkv:
                for i, w in enumerate((Wq_d, Wk_d, Wv_d, Wg_d)):
                    sp.dma_start(W4[:, i, :, :], w.rearrange("(c p) n -> p c n", p=P)).then_inc(s["w_in"], 16)
                sp.dma_start(bg[:], bg_col).then_inc(s["w_in"], 16)
                sp.dma_start(hs[:], hs_col).then_inc(s["w_in"], 16)
                sp.dma_start(mraw[:], mem_kT).then_inc(s["w_in"], 16)
            with sp.Fori(0, B) as b:
                for u in range(U):
                    if u == 0:
                        for v in range(U):
                            sp.dma_start(X[:, v], src[b, v * MACRO:(v + 1) * MACRO].rearrange(
                                "(t p) d -> p t d", p=P)).then_inc(s["x_in"][v], 16)
                    sp.wait_ge(s["res"], (u + 1) * TT)
                    sp.dma_start(dst[b, u * MACRO:(u + 1) * MACRO].rearrange("(t p) d -> p t d", p=P),
                                 X[:, u]).then_inc(s["stored"][u], 16)
                    if qkv:
                        tok = slice(u * MACRO, (u + 1) * MACRO)
                        for c in range(QC):
                            sp.wait_ge(s["qk"], u * QC + c + 1)
                            sp.dma_start((qd if c < HP else kd)[b, :, c % HP, tok],
                                         qn[:, c % 2, :]).then_inc(s["qk_st"][c % 2], 16)
                            if c % 2 == 1:
                                v = c // 2
                                sp.wait_ge(s["v_out"], u * VC + v + 1)
                                t, h = v // 2, v % 2
                                sp.dma_start(vd[b, u * MACRO + t * P:u * MACRO + (t + 1) * P,
                                                h * 512:(h + 1) * 512],
                                             vo[:, v % 2, :]).then_inc(s["v_st"][v % 2], 16)
                        for c in range(HP):
                            sp.wait_ge(s["gs"], u * HP + c + 1)
                            sp.dma_start(gd[b, :, c, tok], gs[:, c % 2, :]).then_inc(s["g_st"][c % 2], 16)
                for v in range(U):
                    sp.wait_ge(s["stored"][v], 16)
                if qkv:
                    for v in range(2):
                        sp.wait_ge(s["qk_st"][v], 16 * U * QC // 2)
                        sp.wait_ge(s["g_st"][v], 16 * U * HP // 2)
                        sp.wait_ge(s["v_st"][v], 16 * U * VC // 2)
                end_round(s, sp, b, leader=True)

        @block.tensor
        def _(pe):
            if not qkv:
                pe.wait_ge(s["ffn_w"], 16)
            if qkv:
                pe.wait_ge(s["w_in"], 112)
                pe.wait_ge(s["memk"], 1)
                nc.tensor.matmul(ps[3][:, 0:HP * MEM], blocks[:], msq[:], start=True, stop=True).then_inc(s["memk"], 1)
            with pe.Fori(0, B) as b:
                for u in range(U):
                    n = u

                    def turn(k):
                        pe.wait_ge(s["xn"], (n * LNS + k + 1) * TT)
                        for c in range(DC):
                            for t in range(TT):
                                last = nc.tensor.transpose(ps[c][:, t * P:(t + 1) * P],
                                                           xn[:, t, c * P:(c + 1) * P], ident[:])
                        last.then_inc(s["tr"], 1)
                        if not qkv and k == 1:
                            return
                        pe.wait_ge(s["xnT"], (n * LNS + k + 1) * DC)

                    if qkv or u == 0:
                        turn(0)
                    else:
                        pe.wait_ge(s["xnT"], (n + 1) * DC)
                    for h in range(FC):
                        if h >= 2:
                            pe.wait_ge(s["gelu"], n * FC + h - 1)
                        for c in range(DC):
                            last = nc.tensor.matmul(ps[2 + h % 2][:], Wfc[:, c, h * P:(h + 1) * P], xnT[:, c, :],
                                                    start=(c == 0), stop=(c == DC - 1))
                        last.then_inc(s["hid"], 1)
                    if not qkv and u + 1 < U:
                        turn(1)
                    pe.wait_ge(s["gelu"], (n + 1) * FC)
                    if n > 0:
                        pe.wait_ge(s["res"], n * TT)
                    for t in range(TT):
                        for h in range(FC):
                            nc.tensor.matmul(ps[4 + t][:, 0:DIM + 1], gT[:, h, t * P:(t + 1) * P], Wp[:, h, :],
                                             start=(h == 0), stop=(h == FC - 1))
                        if t == 0:
                            pe.wait_ge(s["gsum"], n + 1)
                        nc.tensor.matmul(ps[4 + t][:, DIM + 1:DIM + 2], g2T[:, 0, t * P:(t + 1) * P], ones[:, 0:1],
                                         start=True, stop=True).then_inc(s["out"], 1)
                    if not qkv:
                        continue
                    turn(1)
                    for c in range(QC + 1):
                        if c < QC:
                            if c >= 4:
                                pe.wait_ge(s["qk"], n * QC + c - 3)
                            for k in range(DC):
                                last = nc.tensor.matmul(ps[QB[c % 4]][:],
                                                        W4[:, c // HP, k, (c % HP) * P:(c % HP + 1) * P],
                                                        xnT[:, k, :], start=(k == 0), stop=(k == DC - 1))
                            last.then_inc(s["proj"], 1)
                        if c >= 1:
                            pe.wait_ge(s["square"], n * QC + c)
                            if c >= 3:
                                pe.wait_ge(s["norm"], n * QC + c - 2)
                            nc.tensor.matmul(ps[2 + (c - 1) % 2][:], blocks[:], sq[:, (c - 1) % 2, :], start=True,
                                             stop=True).then_inc(s["ssq"], 1)
                        if c < QC and c % 2 == 1:
                            v = c // 2
                            t, h = v // 2, v % 2
                            if v >= 2:
                                pe.wait_ge(s["v_out"], n * VC + v - 1)
                            for k in range(DC):
                                last = nc.tensor.matmul(ps[6 + v % 2][:], xnT[:, k, t * P:(t + 1) * P],
                                                        W4[:, 2, k, h * 512:(h + 1) * 512], start=(k == 0),
                                                        stop=(k == DC - 1))
                            last.then_inc(s["val"], 1)
                    for c in range(HP):
                        if c < 2:
                            pe.wait_ge(s["v_out"], (n + 1) * VC)
                        else:
                            pe.wait_ge(s["sig"], n * HP + c - 1)
                        for k in range(DC):
                            last = nc.tensor.matmul(ps[6 + c % 2][:], W4[:, 3, k, c * P:(c + 1) * P], xnT[:, k, :],
                                                    start=(k == 0), stop=(k == DC - 1))
                        last.then_inc(s["gate"], 1)
                    pe.wait_ge(s["qk"], (n + 1) * QC)
                end_round(s, pe, b)

        @block.scalar
        def _(act):
            if qkv:
                act.wait_ge(s["w_in"], 112)
                nc.scalar.activation(msq[:], mraw[:], ACT.Square).then_inc(s["memk"], 1)
                act.wait_ge(s["memk"], 2)
                nc.scalar.activation(mrt[:], ps[3][:, 0:HP * MEM], ACT.Sqrt).then_inc(s["memk"], 1)
            with act.Fori(0, B) as b:
                for u in range(U):
                    n = u

                    def norm(k):
                        act.wait_ge(s["stat"], (n * LNS + k + 1))
                        nc.scalar.activation(f["std"][:], f["mv"][:, :, 1], ACT.Sqrt,
                                             bias=eps[:, 0:1]).then_inc(s["std"], 1)
                        act.wait_ge(s["tr"], n * LNS + k + 1)
                        for c in range(DC):
                            nc.scalar.activation(xnT[:, c, :], ps[c][:], ACT.Copy).then_inc(s["xnT"], 1)

                    if qkv or u == 0:
                        norm(0)
                    for h in range(FC):
                        act.wait_ge(s["hid"], n * FC + h + 1)
                        nc.scalar.activation(gT[:, h, :], ps[2 + h % 2][:], ACT.Gelu).then_inc(s["gelu"], 1)
                    if not qkv and u + 1 < U:
                        norm(1)
                    act.wait_ge(s["hstat"], n + 1)
                    nc.scalar.activation(f["hstd"][:], f["nv"][:], ACT.Sqrt, bias=eps[:, 0:1],
                                         scale=-1.0).then_inc(s["hstd"], 1)
                    if not qkv:
                        continue
                    norm(1)
                    for c in range(QC + 1):
                        if c < QC:
                            act.wait_ge(s["proj"], n * QC + c + 1)
                            if c >= 2:
                                act.wait_ge(s["ssq"], n * QC + c - 1)
                            nc.scalar.activation(sq[:, c % 2, :], ps[QB[c % 4]][:], ACT.Square).then_inc(s["square"], 1)
                        if c >= 1:
                            act.wait_ge(s["ssq"], n * QC + c)
                            if c >= 3:
                                act.wait_ge(s["qk"], n * QC + c - 2)
                            nc.scalar.activation(rt[:, (c - 1) % 2, :], ps[2 + (c - 1) % 2][:],
                                                 ACT.Sqrt).then_inc(s["norm"], 1)
                        if c < QC and c % 2 == 1:
                            v = c // 2
                            act.wait_ge(s["val"], n * VC + v + 1)
                            if v >= 2:
                                act.wait_ge(s["v_st"][v % 2], 16 * (n * (VC // 2) + v // 2))
                            nc.scalar.activation(vo[:, v % 2, :], ps[6 + v % 2][:], ACT.Copy).then_inc(s["v_out"], 1)
                    act.wait_ge(s["v_st"][0], 16 * (n + 1) * (VC // 2))
                    act.wait_ge(s["v_st"][1], 16 * (n + 1) * (VC // 2))
                    for c in range(HP):
                        act.wait_ge(s["gate"], n * HP + c + 1)
                        if c >= 2:
                            act.wait_ge(s["gs"], n * HP + c - 1)
                        nc.scalar.activation(sg[:, c % 2, :], ps[6 + c % 2][:], ACT.Sigmoid,
                                             bias=bg[:, c:c + 1]).then_inc(s["sig"], 1)
                end_round(s, act, b)

        @block.gpsimd
        def _(pool):
            with pool.Fori(0, B) as b:
                for u in range(U):
                    n = u
                    for h in range(FC):
                        pool.wait_ge(s["gelu"], n * FC + h + 1)
                        nc.gpsimd.tensor_tensor(g2T[:, h, :], gT[:, h, :], gT[:, h, :], ALU.mult).then_inc(s["sq"], 1)
                    if not qkv:
                        continue
                    for c in range(HP):
                        pool.wait_ge(s["sig"], n * HP + c + 1)
                        if c >= 2:
                            pool.wait_ge(s["g_st"][c % 2], 16 * (n * (HP // 2) + c // 2))
                        nc.gpsimd.tensor_scalar(gs[:, c % 2, :], sg[:, c % 2, :], hs[:, c:c + 1], None,
                                                ALU.mult).then_inc(s["gs"], 1)
                    pool.wait_ge(s["g_st"][0], 16 * (n + 1) * (HP // 2))
                    pool.wait_ge(s["g_st"][1], 16 * (n + 1) * (HP // 2))
                end_round(s, pool, b)

        @block.vector
        def _(dve):

            count = [0]

            def link(ins):
                count[0] += 1
                ins.then_inc(s["link"], 1)
                dve.wait_ge(s["link"], count[0])

            if not qkv:
                dve.wait_ge(s["ffn_w"], 16)
            if qkv:
                dve.wait_ge(s["memk"], 3)
                nc.vector.tensor_scalar(mrt[:], mrt[:], L2_EPS, None, ALU.max).then_inc(s["mem"], 1)
                dve.wait_ge(s["mem"], 1)
                nc.vector.reciprocal(msq[:], mrt[:]).then_inc(s["mem"], 1)
                dve.wait_ge(s["mem"], 2)
                nc.vector.tensor_tensor(mkT[:], mraw[:], msq[:], ALU.mult)
            with dve.Fori(0, B) as b:
                for u in range(U):
                    n = u

                    def norm(k):
                        v = u if qkv else u + k
                        for t in range(TT):
                            link(nc.vector.bn_stats(f["bn"][:, t, :], X[:, v, t, :]))
                            link(nc.vector.bn_aggr(f["mv"][:, t, :], f["bn"][:, t, :]))
                        dve.sem_inc(s["stat"], 1)
                        dve.wait_ge(s["std"], n * LNS + k + 1)
                        link(nc.vector.reciprocal(f["rstd"][:], f["std"][:]))
                        for t in range(TT):
                            nc.vector.tensor_scalar(xn[:, t, :], X[:, v, t, :], f["mv"][:, t, 0:1],
                                                    f["rstd"][:, t:t + 1], ALU.subtract, ALU.mult).then_inc(s["xn"], 1)

                    if qkv or u == 0:
                        dve.wait_ge(s["x_in"][u], 16)
                        norm(0)
                    for h in range(1, FC):
                        dve.wait_ge(s["sq"], n * FC + h + 1)
                        last = nc.vector.tensor_tensor(g2T[:, 0, :], g2T[:, 0, :], g2T[:, h, :], ALU.add)
                        if h < FC - 1:
                            link(last)
                    last.then_inc(s["gsum"], 1)
                    if not qkv and u + 1 < U:
                        dve.wait_ge(s["x_in"][u + 1], 16)
                        dve.wait_ge(s["tr"], n + 1)
                        norm(1)
                    for t in range(TT):
                        dve.wait_ge(s["out"], n * TT + t + 1)
                        link(nc.vector.tensor_scalar(f["st"][:, t, :], ps[4 + t][:, DIM:DIM + 2], 1.0 / HID, None,
                                                     ALU.mult))
                    link(nc.vector.tensor_scalar(f["nmu"][:], f["st"][:, :, 0], -1.0, None, ALU.mult))
                    link(nc.vector.tensor_tensor(f["nv"][:], f["st"][:, :, 0], f["st"][:, :, 0], ALU.mult))
                    nc.vector.tensor_tensor(f["nv"][:], f["nv"][:], f["st"][:, :, 1],
                                            ALU.subtract).then_inc(s["hstat"], 1)
                    dve.wait_ge(s["hstd"], n + 1)
                    link(nc.vector.reciprocal(f["hrstd"][:], f["hstd"][:]))
                    for t in range(TT):
                        link(nc.vector.scalar_tensor_tensor(out=f["t1"][:, t], in0=Bsum, scalar=f["nmu"][:, t:t + 1],
                                                            in1=ps[4 + t][:, 0:DIM], op0=ALU.mult, op1=ALU.add))
                        link(nc.vector.scalar_tensor_tensor(out=f["t2"][:, t], in0=f["t1"][:, t],
                                                            scalar=f["hrstd"][:, t:t + 1], in1=Csum,
                                                            op0=ALU.mult, op1=ALU.add))
                        nc.vector.scalar_tensor_tensor(out=X[:, u, t], in0=f["t2"][:, t], scalar=0.5,
                                                       in1=X[:, u, t], op0=ALU.mult, op1=ALU.add).then_inc(s["res"], 1)
                    dve.wait_ge(s["res"], (n + 1) * TT)
                    if qkv:
                        norm(1)
                        for c in range(QC):
                            dve.wait_ge(s["norm"], n * QC + c + 1)
                            link(nc.vector.tensor_scalar(rr[:, c % 2, :], rt[:, c % 2, :], L2_EPS, None, ALU.max))
                            link(nc.vector.reciprocal(ri[:, c % 2, :], rr[:, c % 2, :]))
                            if c >= 2:
                                dve.wait_ge(s["qk_st"][c % 2], 16 * (n * (QC // 2) + c // 2))
                            nc.vector.scalar_tensor_tensor(out=qn[:, c % 2, :], in0=ps[QB[c % 4]][:],
                                                           scalar=QK_SCALE if c < HP else 1.0, in1=ri[:, c % 2, :],
                                                           op0=ALU.mult, op1=ALU.mult).then_inc(s["qk"], 1)
                        dve.wait_ge(s["qk_st"][0], 16 * (n + 1) * (QC // 2))
                        dve.wait_ge(s["qk_st"][1], 16 * (n + 1) * (QC // 2))
                end_round(s, dve, b)


def attention(nc, ps, mkT, ones, qd, kd, gd, vd, x1d, x2d, sd, pre_th, post_th, mem_v, Wo_d, delta_c, mask_c,
              guess_c):
    S = IB * TPB
    MPC = [len(pieces(width(s // TPB))) for s in range(S)]
    MCUM = [sum(MPC[:s]) for s in range(S + 1)]
    HPC = [len(pieces(width(k // H))) for k in range(IB * H)]
    HCUM = [sum(HPC[:k]) for k in range(IB * H + 1)]
    HSTEPS = 14
    HEADS = [range(H * t // HSTEPS, H * (t + 1) // HSTEPS) if t < HSTEPS else range(0) for t in range(TPB)]
    PG = [-(-(s // TPB + 1) // 4) + 1 for s in range(S)]
    PCUM = [sum(PG[:s]) for s in range(S + 1)]
    SNR = 2
    G0 = 4

    def score_slot(k):
        if k < H:
            return k // G0 % SNR, k % G0 * width(0), k // G0 // SNR
        return k % SNR, 0, H // G0 // SNR + (k - H) // SNR

    FAST = FAST_IB * TPB
    SHARE = IB // 2 * TPB
    SQ = [(i - FAST + 1 if i >= FAST and k == 0 else 0) for i in range(S) for k in range(MPC[i])]
    TWO = IB // 2 - 1
    ATO = [(TWO + 1) * (hb % 2) if hb // 2 < TWO else 0 for hb in range(2 * IB)]

    with ExitStack() as ctx:
        def sb(name, shape, dt=F32):
            return ctx.enter_context(nc.sbuf_tensor(name, shape, dt))
        kT = sb("kT", [P, HP, JW])
        V = sb("V", [P, IB, INNER])
        vm = sb("vm", [MEM, INNER])
        qT = sb("qT", [P, 2, HP, P])
        gT = sb("gateT", [P, HP, P])
        Sn = sb("Sn", [P, SNR, JW])
        Sg = sb("Sg", [P, DRING, JW])
        D = sb("D", [P, RING, JW])
        SG = sb("SG", [P, 2, JW])
        W = sb("W", [P, 2, JW])
        junk = sb("junk", [P, JW], mybir.dt.bfloat16)
        E = sb("E", [P, 2, JW])
        AT = sb("AT", [P, IB + 1, H, P // 2])
        UT = sb("UT", [P, HP, P])
        Wo = sb("Wo", [P, HP, DIM])
        x1 = sb("x1", [P, 2, DIM])
        x2 = sb("x2", [P, 2, DIM])
        delta = sb("delta", [P, P])
        wrep = sb("wrep", [P, 2, H])
        kpre = sb("kpre", [P, H, R8])
        kpost = sb("kpost", [P, H, R8])
        kr = sb("kr", [P, 2, H * R8])
        mask = sb("mask", [P, 2 * P - R8])
        top8 = sb("top8", [P, TOPK])
        guess = sb("guess", [P, 3, IB * TPB])
        iota8 = sb("iota8", [P, 8])
        half = sb("half", [P, 1])
        rmax = sb("rmax", [P, RING])
        nmax = sb("nmax", [P, RING])
        sums = sb("sums", [P, RING, 2])
        mom = sb("mom", [P, 6])
        dev = sb("dev", [P, RING])
        nt = sb("nt", [P, RING, 3])
        cnt = sb("cnt", [P, RING, 3])
        upd = sb("upd", [P, 2])
        w = sb("w", [P, RING, 4])
        m8 = sb("m8", [P, RING, 8])
        pick = sb("pick", [P, RING])
        vk = sb("vk", [P, RING])
        bad = sb("bad", [P, RING, 3])
        flag = sb("flag", [1, 2], mybir.dt.int32)
        rs = sb("rs", [P, 2])
        ri = sb("rinv", [P, 2])
        s = semaphores(nc, ctx, "t", dict(c_in=1, kpre=1, konst=1, k_in=IB, v_in=IB, q_in=2, g_in=1, mem_k=1, s_ps=1, s_sb=1,
                                    s_st=SNR, sg_in=DRING, mixed=1, d_raw=1, d_ok=1, rmax=1, nm=1, exp=1, sums=1, nt0=1, nt1=1, nt2=1,
                                    cnt1=1, cnt2=1, cnt3=1, prep=1, side=1, v=1, pick=1, vk=1, bad=1, any=1, flag=1, prob=1,
                                    link=1, general=1, chain=1,
                                    rinv=1, kr=1, post=1, at=1, av=1, ut=1, y=1, x_in=2, x_ok=1,
                                    x_st=2), keep=("c_in", "kpre", "konst", "general"))
        block = ctx.enter_context(nc.Block())

        @block.sync
        def _(sp):
            sp.dma_start(delta[:], delta_c).then_inc(s["c_in"], 16)
            sp.dma_start(mask[:], mask_c).then_inc(s["c_in"], 16)
            sp.dma_start(guess[:], guess_c).then_inc(s["c_in"], 16)
            sp.dma_start(Wo[:], Wo_d.rearrange("(c p) n -> p c n", p=P)).then_inc(s["c_in"], 16)
            sp.dma_start(vm[:], mem_v).then_inc(s["c_in"], 16)
            for i, th in enumerate((pre_th, post_th)):
                for g in range(H):
                    sp.dma_start(wrep[g * R8:(g + 1) * R8, i, :],
                                 th[g:g + 1, :].broadcast_to([R8, H])).then_inc(s["c_in"], 16)
            with sp.Fori(0, B) as b:
                def keys(ib):
                    r = slice(ib * P, (ib + 1) * P)
                    sp.dma_start(kT[:, :, MEM + ib * P:MEM + (ib + 1) * P], kd[b, :, :, r]).then_inc(s["k_in"][ib], 16)
                    if ib >= 2:
                        sp.wait_ge(s["s_ps"], HCUM[H * (ib - 1)])
                    sp.dma_start(qT[:, ib % 2], qd[b, :, :, r]).then_inc(s["q_in"][ib % 2], 16)

                def late(ib):
                    r = slice(ib * P, (ib + 1) * P)
                    sp.dma_start(V[:, ib, :], vd[b, r, :]).then_inc(s["v_in"][ib], 16)
                    if ib >= 1:
                        sp.wait_ge(s["ut"], 2 * ib)
                    sp.dma_start(gT[:], gd[b, :, :, r]).then_inc(s["g_in"], 16)
                    if ib >= 2:
                        sp.wait_ge(s["x_ok"], ib - 1)
                    sp.dma_start(x1[:, ib % 2], x1d[b, r, :]).then_inc(s["x_in"][ib % 2], 16)

                def store(ib, h):
                    k = ib * H + h
                    n = width(ib)
                    if ib == 0:
                        sp.wait_ge(s["s_sb"], HCUM[k + G0])
                        slot = score_slot(k)[0]
                        sp.dma_start(sd[0, h:h + G0, :, 0:n].rearrange("h r n -> r h n"),
                                     Sn[:, slot, 0:G0 * n].rearrange("p (h n) -> p h n", h=G0)).then_inc(
                                         s["s_st"][slot], 16)
                        return
                    sp.wait_ge(s["s_sb"], HCUM[k + 1])
                    sp.dma_start(sd[ib % 2, h, :, 0:n], Sn[:, k % SNR, 0:n]).then_inc(s["s_st"][k % SNR], 16)

                def load(i):
                    ib, t = i // TPB, i % TPB
                    n = width(ib)
                    if t == 0:
                        for v in range(SNR):
                            sp.wait_ge(s["s_st"][v], 16 * (H // G0 // SNR + H * ib // SNR))
                    if i >= DRING:
                        sp.wait_ge(s["mixed"], MCUM[i - DRING + 1])
                    sp.dma_start(Sg[:, i % DRING, 0:n],
                                 sd[ib % 2, :, t * R8:(t + 1) * R8, 0:n]).then_inc(s["sg_in"][i % DRING], 16)

                keys(0)
                for h in range(0, H, G0):
                    store(0, h)
                keys(1)
                late(0)
                for i in range(DRING):
                    load(i)
                for i in range(S):
                    ib, t = i // TPB, i % TPB
                    if ib + 1 < IB:
                        for h in HEADS[t]:
                            store(ib + 1, h)
                    if i + DRING < S:
                        load(i + DRING)
                    if t == 10 and ib >= 1:
                        sp.wait_ge(s["x_ok"], ib)
                        sp.dma_start(x2d[b, (ib - 1) * P:ib * P, :],
                                     x2[:, (ib - 1) % 2]).then_inc(s["x_st"][(ib - 1) % 2], 16)
                    if t == 8 and ib + 2 < IB:
                        keys(ib + 2)
                    if t == 8 and ib >= 1:
                        late(ib)
                sp.wait_ge(s["x_ok"], IB)
                sp.dma_start(x2d[b, (IB - 1) * P:IB * P, :],
                             x2[:, (IB - 1) % 2]).then_inc(s["x_st"][(IB - 1) % 2], 16)
                for v in range(2):
                    sp.wait_ge(s["x_st"][v], 16 * IB // 2)
                end_round(s, sp, b, leader=True)

        @block.tensor
        def _(pe):
            pe.wait_ge(s["c_in"], 16 * (5 + 2 * H))
            pe.wait_ge(s["kpre"], 2)
            with pe.Fori(0, B) as b:
                def scores(ib, h):
                    k = ib * H + h
                    if h == 0:
                        pe.wait_ge(s["k_in"][ib], 16)
                        if ib == 0:
                            pe.wait_ge(s["mem_k"], 1)
                        pe.wait_ge(s["q_in"][ib % 2], 16 * (ib // 2 + 1))
                    lo = DH * (h % 2)
                    for i, (c0, c1) in enumerate(pieces(width(ib))):
                        m = HCUM[k] + i
                        if m >= 2:
                            pe.wait_ge(s["s_sb"], m - 1)
                        nc.tensor.matmul(ps[m % 2][:, 0:c1 - c0], qT[lo:lo + DH, ib % 2, h // 2, :],
                                         kT[lo:lo + DH, h // 2, c0:c1], start=True, stop=True).then_inc(s["s_ps"], 1)

                def mix(i, rest):
                    if not rest:
                        pe.wait_ge(s["sg_in"][i % DRING], 16 * (i // DRING + 1))
                    for k, (c0, c1) in enumerate(pieces(width(i // TPB))):
                        if (k >= 2) != rest:
                            continue
                        m = MCUM[i] + k
                        if m >= 2:
                            pe.wait_ge(s["d_raw"], m - 1)
                        if m >= 2 and SQ[m - 2] > 0:
                            pe.wait_ge(s["sums"], SQ[m - 2])
                        nc.tensor.matmul(ps[2 + m % 2][:, 0:c1 - c0], kpre[:].rearrange("p h r -> p (h r)"),
                                         Sg[:, i % DRING, c0:c1], start=True, stop=True).then_inc(s["mixed"], 1)

                def post(i):
                    ib = i // TPB
                    pe.wait_ge(s["prob"], i + 1)
                    pe.wait_ge(s["kr"], i + 1)
                    for g in range(PG[i]):
                        m = PCUM[i] + g
                        free = bank_free(i, g)
                        if free > 0:
                            pe.wait_ge(s["at"], free)
                        bank = ps[7 if g == 0 else 4 + g % 2]
                        if g == 0:
                            last = nc.tensor.matmul(bank[0:MEM, 0:P], E[:, i % 2, 0:MEM], kr[:, i % 2, :],
                                                    start=True, stop=True)
                        else:
                            for c in range(4 * (g - 1), min(4 * g, ib + 1)):
                                last = nc.tensor.matmul(bank[:, (c % 4) * P:(c % 4 + 1) * P],
                                                        E[:, i % 2, MEM + c * P:MEM + (c + 1) * P],
                                                        kr[:, i % 2, :], start=True, stop=True)
                        last.then_inc(s["post"], 1)

                def bank_free(i, g):
                    for j in range(i, -1, -1):
                        for f in reversed(range(PG[j])):
                            if (j < i or f < g) and (f == g == 0 or (f * g > 0 and f % 2 == g % 2)):
                                return PCUM[j] + f + 1
                    return 0

                def any_bad(i):
                    n = i - FAST
                    pe.wait_ge(s["bad"], n + 1)
                    if n >= 1:
                        pe.wait_ge(s["flag"], n)
                    nc.tensor.matmul(ps[7][64:65, 0:1], bad[:, i % RING, 0:1], ones[:, 0:1], start=True,
                                     stop=True).then_inc(s["any"], 1)

                def values(hb, part):
                    ib = hb // 2
                    if part == 0:
                        pe.wait_ge(s["at"], PCUM[(hb + 1) * TPH])
                        if hb % 2 == 0:
                            pe.wait_ge(s["v_in"][ib], 16)
                        if hb >= 1:
                            pe.wait_ge(s["ut"], hb)
                        if hb % 2 == 0 and hb >= 2:
                            pe.wait_ge(s["x_ok"], ib)
                    for h in range(part * H // 2, (part + 1) * H // 2):
                        lo = DH * (h % 2)
                        dst = ps[6][lo:lo + DH, (h // 2) * DH:(h // 2 + 1) * DH]
                        for c in range(ib + 1):
                            nc.tensor.matmul(dst, V[:, c, h * DH:(h + 1) * DH], AT[:, c + ATO[hb], h, :],
                                             start=(c == 0), stop=False)
                        last = nc.tensor.matmul(dst, vm[:, h * DH:(h + 1) * DH], AT[0:MEM, ATO[hb] + ib + 1, h, :], start=False,
                                                stop=True)
                    if part == 1:
                        last.then_inc(s["av"], 1)

                def project(ib):
                    pe.wait_ge(s["ut"], 2 * (ib + 1))
                    for p in range(HP):
                        last = nc.tensor.matmul(ps[6][:, 0:DIM], UT[:, p, :], Wo[:, p, :], start=(p == 0),
                                                stop=(p == HP - 1))
                    last.then_inc(s["y"], 1)

                for h in range(H):
                    scores(0, h)
                mix(0, False)
                for k in range(S + 9):
                    ib, t = k // TPB, k % TPB
                    heads = HEADS[t] if ib + 1 < IB else range(0)
                    if k < S:
                        mix(k, True)
                    for h in heads[:1]:
                        scores(ib + 1, h)
                    if k + 1 < S:
                        mix(k + 1, False)
                    for h in heads[1:]:
                        scores(ib + 1, h)
                    if FAST + 4 <= k < S + 4:
                        any_bad(k - 4)
                    if k >= 14 and (k - 14) % TPH == 0:
                        values((k - 14) // TPH, 1)
                    if 5 <= k < S + 5:
                        post(k - 5)
                    if k >= 13 and (k - 13) % TPH == 0:
                        values((k - 13) // TPH, 0)
                    if k >= 24 and (k - 24) % TPB == 0:
                        project((k - 24) // TPB)
                end_round(s, pe, b)

        @block.scalar
        def _(act):
            with act.Fori(0, B) as b:
                def mixed(i):
                    if i >= RING:
                        act.wait_ge(s["prob"], i - RING + 1)
                    for k, (c0, c1) in enumerate(pieces(width(i // TPB))):
                        m = MCUM[i] + k
                        act.wait_ge(s["mixed"], m + 1)
                        src, dst = ps[2 + m % 2][:, 0:c1 - c0], D[:, i % RING, c0:c1]
                        if i >= FAST and k == 0:
                            nc.scalar.activation(dst, src, ACT.Identity,
                                                 accum_out=sums[:, i % RING, 0:1]).then_inc(s["d_raw"], 1)
                            if i == FAST + 1:
                                act.wait_ge(s["sums"], 1)
                            elif i == FAST + 2:
                                act.wait_ge(s["cnt1"], 1)
                            elif i >= FAST + 3:
                                act.wait_ge(s["cnt2"], i - 3 - FAST + 1)
                            nc.scalar.activation(junk[:, 0:c1 - c0], src, ACT.Square, scale=1.0 / math.sqrt(c1 - c0),
                                                 accum_out=sums[:, i % RING, 1:2]).then_inc(s["sums"], 1)
                        else:
                            nc.scalar.activation(dst, src, ACT.Copy).then_inc(s["d_raw"], 1)

                def count(i, r):
                    n, o = width(i // TPB), i - FAST
                    act.wait_ge(s[f"nt{r}"], o + 1)
                    if r == 0:
                        act.wait_ge(s["d_ok"], i + 1)
                        act.wait_ge(s["sums"], min(o + 2, S - FAST))
                    if r == 1:
                        act.wait_ge(s["cnt1"], min(o + 2, S - FAST))
                    if r == 2 and o >= 2:
                        act.wait_ge(s["pick"], o - 1)
                    out = SG[:, i % 2, 0:n] if r == 2 else junk[:, 0:n]
                    nc.scalar.activation(out, D[:, i % RING, 0:n], ACT.Sign, bias=nt[:, i % RING, r:r + 1],
                                         accum_out=cnt[:, i % RING, r:r + 1]).then_inc(s[f"cnt{r + 1}"], 1)

                def exps(i):
                    n = width(i // TPB)
                    act.wait_ge(s["nm"], i + 1)
                    if i >= 2:
                        act.wait_ge(s["post"], PCUM[i - 1])
                    nc.scalar.activation(E[:, i % 2, 0:n], D[:, i % RING, 0:n], ACT.Exp,
                                         bias=nmax[:, i % RING:i % RING + 1]).then_inc(s["exp"], 1)

                def turned(i):
                    ib, t, hb = i // TPB, i % TPH, i // TPH
                    need = hb - 1 if ib < TWO else hb
                    if t == 0 and need >= 1:
                        act.wait_ge(s["av"], need)
                    for g in range(PG[i]):
                        m = PCUM[i] + g
                        act.wait_ge(s["post"], m + 1)
                        bank = ps[7 if g == 0 else 4 + g % 2]
                        if g == 0:
                            dst = AT[0:MEM, ATO[hb] + ib + 1, :, t * R8:(t + 1) * R8]
                            src = bank[0:MEM, 0:P].rearrange("p (h r) -> p h r", h=H)
                        else:
                            c0, c1 = 4 * (g - 1), min(4 * g, ib + 1)
                            dst = AT[:, c0 + ATO[hb]:c1 + ATO[hb], :, t * R8:(t + 1) * R8]
                            src = bank[:, 0:(c1 - c0) * P].rearrange("p (c h r) -> p c h r", h=H, r=R8)
                        nc.scalar.activation(dst, src, ACT.Copy).then_inc(s["at"], 1)

                for k in range(S + 6):
                    if FAST + 3 <= k < S + 3:
                        count(k - 3, 2)
                    if k < S:
                        mixed(k)
                    if k >= 6 and (k - 6) % TPH > 0:
                        turned(k - 6)
                    if FAST + 1 <= k < S + 1:
                        count(k - 1, 0)
                    if FAST + 2 <= k < S + 2:
                        count(k - 2, 1)
                    if 4 <= k < S + 4:
                        exps(k - 4)
                    if k >= 6 and (k - 6) % TPH == 0:
                        turned(k - 6)
                end_round(s, act, b)

        @block.gpsimd
        def _(pool):
            pool.wait_ge(s["c_in"], 16 * (5 + 2 * H))
            for i, k in enumerate((kpre, kpost)):
                for h in range(H):
                    last = nc.gpsimd.tensor_scalar(k[:, h, :], delta[:, 0:R8], wrep[:, i, h:h + 1], None, ALU.mult)
                last.then_inc(s["kpre"], 1)
            nc.gpsimd.memset(half[:], 0.5)
            nc.gpsimd.iota(iota8[:], [[1, 8]], base=0, channel_multiplier=0, allow_small_or_imprecise_dtypes=True).then_inc(s["konst"], 1)
            pool.wait_ge(s["kpre"], 2)
            with pool.Fori(0, B) as b:
                nc.gpsimd.tensor_copy(kT[:, :, 0:MEM], mkT[:].rearrange("p (c m) -> p c m", c=HP)).then_inc(
                    s["mem_k"], 1)
                links = [0]

                def chain(ins):
                    links[0] += 1
                    ins.then_inc(s["chain"], 1)
                    pool.wait_ge(s["chain"], links[0])

                ts, tt = nc.gpsimd.tensor_scalar, nc.gpsimd.tensor_tensor

                def causal(i):
                    ib, t = i // TPB, i % TPB
                    n = width(ib)
                    pool.wait_ge(s["d_raw"], MCUM[i + 1])
                    d = D[:, i % RING, n - P:n]
                    tt(d, d, mask[:, P - R8 - R8 * t:2 * P - R8 - R8 * t], ALU.add).then_inc(s["d_ok"], 1)

                def first_guess(i):
                    e, n = i % RING, pieces(width(i // TPB))[0][1]
                    pool.wait_ge(s["sums"], i - FAST + 1)
                    if i > FAST:
                        pool.wait_ge(s["nt0"], i - FAST)
                    chain(ts(mom[:, 0:1], sums[:, e, 0:1], -1.0 / n, None, ALU.mult))
                    chain(ts(mom[:, 3:4], mom[:, 0:1], mom[:, 0:1], sums[:, e, 1:2], ALU.mult,
                             ALU.subtract))
                    chain(ts(mom[:, 5:6], mom[:, 3:4], -1.0, 0.0, ALU.mult, ALU.max))
                    chain(tt(dev[:, e:e + 1], mom[:, 5:6], half[:], ALU.pow))
                    ts(nt[:, e, 0:1], dev[:, e:e + 1], guess[:, 0, i:i + 1], mom[:, 0:1], ALU.mult,
                       ALU.add).then_inc(s["nt0"], 1)

                def better(i, r):
                    e, n = i % RING, width(i // TPB)
                    pool.wait_ge(s[f"cnt{r}"], i - FAST + 1)
                    if i > FAST:
                        pool.wait_ge(s[f"nt{r}"], i - FAST)
                    chain(ts(upd[:, r - 1:r], cnt[:, e, r - 1:r], float(n - 2 * TOPK + 1), dev[:, e:e + 1], ALU.add,
                             ALU.mult))
                    ts(nt[:, e, r:r + 1], upd[:, r - 1:r], guess[:, r, i:i + 1], nt[:, e, r - 1:r], ALU.mult,
                       ALU.add).then_inc(s[f"nt{r}"], 1)

                def prepare(i):
                    e, n = i % RING, width(i // TPB)
                    o = i - FAST
                    pool.wait_ge(s["cnt3"], o + 1)
                    pool.wait_ge(s["prob"], i - 3)
                    chain(ts(w[:, e, 0:1], cnt[:, e, 2:3], float(2 * TOPK - 1 - n), -2.0, ALU.is_gt, ALU.mult))
                    ts(w[:, e, 1:2], w[:, e, 0:1], 1.0, None, ALU.add).then_inc(s["side"], 1)
                    pool.wait_ge(s["side"], o + 1)
                    if i >= SHARE:
                        pool.wait_ge(s["prob"], i - 1)
                        ts(W[:, i % 2, 0:n], D[:, i % RING, 0:n], w[:, e, 1:2], SMALL, ALU.mult,
                           ALU.mult).then_inc(s["v"], 1)
                    chain(ts(w[:, e, 2:3], cnt[:, e, 2:3], float(n - 2 * TOPK + 1), w[:, e, 1:2], ALU.add, ALU.mult))
                    ts(w[:, e, 3:4], w[:, e, 2:3], -0.5, -0.5, ALU.mult, ALU.add).then_inc(s["prep"], 1)

                def judge(i):
                    e, o = i % RING, i - FAST
                    pool.wait_ge(s["pick"], o + 1)
                    chain(ts(bad[:, e, 2:3], m8[:, e, 0:1], w[:, e, 1:2], 1.0 / SMALL, ALU.mult, ALU.mult))
                    chain(ts(bad[:, e, 1:2], bad[:, e, 2:3], nt[:, e, 2:3], 0.0, ALU.add, ALU.is_equal))
                    ts(bad[:, e, 0:1], w[:, e, 2:3], -15.5, bad[:, e, 1:2], ALU.is_lt,
                       ALU.add).then_inc(s["bad"], 1)

                def spread(i):
                    pool.wait_ge(s["rinv"], i + 1)
                    if i >= 2:
                        pool.wait_ge(s["post"], PCUM[i - 1])
                    ts(kr[:, i % 2, :], kpost[:].rearrange("p h r -> p (h r)"), ri[:, i % 2:i % 2 + 1], 1.0,
                       ALU.mult, ALU.mult).then_inc(s["kr"], 1)

                for k in range(S + 5):
                    if k >= 5:
                        spread(k - 5)
                    if FAST + 3 <= k < S + 3:
                        prepare(k - 3)
                    if k < S:
                        causal(k)
                    if FAST + 1 <= k < S + 1:
                        better(k - 1, 1)
                    if FAST + 2 <= k < S + 2:
                        better(k - 2, 2)
                    if FAST <= k < S:
                        first_guess(k)
                    if FAST + 3 <= k < S + 3:
                        judge(k - 3)
                end_round(s, pool, b)

        @block.vector
        def _(dve):
            dve.wait_ge(s["konst"], 1)
            with dve.Fori(0, B) as b:
                links = [0]

                def link(ins):
                    links[0] += 1
                    ins.then_inc(s["link"], 1)
                    dve.wait_ge(s["link"], links[0])

                def scores(ib, h):
                    k = ib * H + h
                    slot, o, before = score_slot(k)
                    if before > 0:
                        dve.wait_ge(s["s_st"][slot], 16 * before)
                    for i, (c0, c1) in enumerate(pieces(width(ib))):
                        m = HCUM[k] + i
                        dve.wait_ge(s["s_ps"], m + 1)
                        nc.vector.tensor_copy(Sn[:, slot, o + c0:o + c1], ps[m % 2][:, 0:c1 - c0]).then_inc(s["s_sb"], 1)

                def row_max(i):
                    dve.wait_ge(s["d_ok"], i + 1)
                    nc.vector.tensor_reduce(rmax[:, i % RING:i % RING + 1], D[:, i % RING, 0:width(i // TPB)],
                                            mybir.AxisListType.X, ALU.max).then_inc(s["rmax"], 1)
                    dve.wait_ge(s["rmax"], i + 1)
                    nc.vector.tensor_scalar(nmax[:, i % RING:i % RING + 1], rmax[:, i % RING:i % RING + 1], -1.0,
                                            None, ALU.mult).then_inc(s["nm"], 1)

                def search(i):
                    e, h, n, o = i % RING, i % 2, width(i // TPB), i - FAST
                    dve.wait_ge(s["side"], o + 1)
                    if i >= SHARE:
                        dve.wait_ge(s["v"], i - SHARE + 1)
                    else:
                        link(nc.vector.tensor_scalar(W[:, h, 0:n], D[:, e, 0:n], w[:, e, 1:2], SMALL, ALU.mult,
                                                     ALU.mult))
                    link(nc.vector.scalar_tensor_tensor(out=W[:, h, 0:n], in0=SG[:, h, 0:n], scalar=w[:, e, 1:2],
                                                        in1=W[:, h, 0:n], op0=ALU.is_equal, op1=ALU.subtract,
                                                        reverse1=True))
                    link(nc.vector.max(m8[:, e, :], W[:, h, 0:n]))
                    dve.wait_ge(s["prep"], o + 1)
                    nc.vector.scalar_tensor_tensor(out=top8[:, 0:8], in0=iota8[:], scalar=w[:, e, 3:4],
                                                   in1=m8[:, e, :], op0=ALU.is_equal, op1=ALU.mult,
                                                   accum_out=pick[:, e:e + 1]).then_inc(s["pick"], 1)
                    dve.wait_ge(s["pick"], o + 1)
                    nc.vector.tensor_scalar(vk[:, e:e + 1], pick[:, e:e + 1], w[:, e, 1:2], 1.0 / SMALL, ALU.mult,
                                            ALU.mult).then_inc(s["vk"], 1)

                def general(i):
                    e, n = i % RING, width(i // TPB)
                    d, rest = D[:, e, 0:n], W[:, i % 2, 0:n]
                    nc.vector.sem_clear(s["general"])
                    count = [0]

                    def step(ins):
                        count[0] += 1
                        ins.then_inc(s["general"], 1)
                        dve.wait_ge(s["general"], count[0])

                    for r in range(TOPK // 8):
                        t8 = top8[:, 8 * r:8 * r + 8]
                        step(nc.vector.max(t8, d if r == 0 else rest))
                        if r < TOPK // 8 - 1:
                            step(nc.vector.match_replace(out=rest, in_to_replace=t8, in_values=d if r == 0 else rest,
                                                         imm_value=NEG))
                    step(nc.vector.tensor_copy(vk[:, e:e + 1], top8[:, TOPK - 1:TOPK]))

                def threshold(i):
                    if MEM + (i + 1) * R8 <= TOPK:
                        link(nc.vector.memset(vk[:, i % RING:i % RING + 1], 2 * MASKED))
                        return
                    if i < FAST:
                        general(i)
                        return
                    dve.wait_ge(s["any"], i - FAST + 1)
                    nc.vector.tensor_copy(flag[0:1, i % 2:i % 2 + 1], ps[7][64:65, 0:1]).then_inc(s["flag"], 1)
                    dve.wait_ge(s["flag"], i - FAST + 1)
                    missed = dve.value_load(flag[0:1, i % 2:i % 2 + 1], min_val=0, max_val=2 * P)
                    dve.wait_ge(s["vk"], i - FAST + 1)
                    with dve.If(missed > 0):
                        general(i)

                def select(i):
                    e, n = i % 2, width(i // TPB)
                    dve.wait_ge(s["exp"], i + 1)
                    if i >= 2:
                        dve.wait_ge(s["kr"], i - 1)
                    nc.vector.scalar_tensor_tensor(out=E[:, e, 0:n], in0=D[:, i % RING, 0:n], scalar=vk[:, i % RING:i % RING + 1],
                                                   in1=E[:, e, 0:n], op0=ALU.is_ge, op1=ALU.mult,
                                                   accum_out=rs[:, e:e + 1]).then_inc(s["prob"], 1)
                    dve.wait_ge(s["prob"], i + 1)
                    nc.vector.reciprocal(ri[:, e:e + 1], rs[:, e:e + 1]).then_inc(s["rinv"], 1)

                def gated(hb):
                    ib = hb // 2
                    dve.wait_ge(s["av"], hb + 1)
                    if hb % 2 == 0:
                        dve.wait_ge(s["g_in"], 16 * (ib + 1))
                        if ib >= 1:
                            dve.wait_ge(s["y"], ib)
                    o = (hb % 2) * (P // 2)
                    nc.vector.tensor_tensor(UT[:, :, o:o + P // 2], ps[6][:].rearrange("p (c r) -> p c r", c=HP),
                                            gT[:, :, o:o + P // 2], ALU.mult).then_inc(s["ut"], 1)

                def residual(ib):
                    dve.wait_ge(s["y"], ib + 1)
                    dve.wait_ge(s["x_in"][ib % 2], 16 * (ib // 2 + 1))
                    if ib >= 2:
                        dve.wait_ge(s["x_st"][ib % 2], 16 * (ib // 2))
                    nc.vector.tensor_tensor(x2[:, ib % 2, :], ps[6][:, 0:DIM], x1[:, ib % 2, :],
                                            ALU.add).then_inc(s["x_ok"], 1)

                for h in range(H):
                    scores(0, h)
                for k in range(S + 9):
                    ib, t = k // TPB, k % TPB
                    heads = HEADS[t] if ib + 1 < IB else range(0)
                    if 5 <= k < S + 5:
                        threshold(k - 5)
                        select(k - 5)
                    for h in heads[:1]:
                        scores(ib + 1, h)
                    if 1 <= k < S + 1:
                        row_max(k - 1)
                    for h in heads[1:]:
                        scores(ib + 1, h)
                    if FAST + 3 <= k < S + 3:
                        search(k - 3)
                    if k >= 14 and (k - 14) % TPH == 0:
                        gated((k - 14) // TPH)
                    if k >= 24 and (k - 24) % TPB == 0:
                        residual((k - 24) // TPB)
                end_round(s, dve, b)


def guess_table():
    table = np.zeros((P, 3, IB * TPB), np.float32)
    for tile in range(FAST_IB * TPB, IB * TPB):
        for r in range(R8):
            keys = MEM + tile * R8 + r + 1
            lo, hi = -8.0, 8.0
            while hi - lo > 1e-9:
                mid = (lo + hi) / 2
                if 0.5 * math.erfc(mid / math.sqrt(2)) * keys > TOPK - 0.5:
                    lo = mid
                else:
                    hi = mid
            density = math.exp(-lo * lo / 2) / math.sqrt(2 * math.pi)
            table[r::R8, 0, tile] = -lo
            for k, damp in enumerate(DAMP):
                table[r::R8, 1 + k, tile] = -0.5 * damp / (keys * density)
    return table


def kernel(L0_attn_x, L0_attn_Wq, L0_attn_Wk, L0_attn_Wv, L0_attn_W_pre_th, L0_attn_W_post_th, L0_attn_mem_k,
           L0_attn_mem_v, L0_attn_head_scale_params, L0_attn_Wg, L0_attn_bg, L0_attn_Wo, L0_ffn_W_fc, L0_ffn_ln_w,
           L0_ffn_ln_b, L0_ffn_W_proj):
    import concourse.bacc as bacc
    from concourse.bass_utils import run_bass_kernel_spmd

    nc = bacc.Bacc("TRN2", target_bir_lowering=False, num_devices=1)
    pair_cols = lambda v: np.asarray(v).reshape(HP, P).T
    head = np.asarray(L0_attn_head_scale_params).reshape(H, 1)
    p = np.arange(P)
    u = np.arange(2 * P - R8)
    layout = dict(
        x=np.asarray(L0_attn_x),
        Wq=np.asarray(L0_attn_Wq), Wk=np.asarray(L0_attn_Wk), Wv=np.asarray(L0_attn_Wv),
        pre_th=np.asarray(L0_attn_W_pre_th).T, post_th=np.asarray(L0_attn_W_post_th).T,
        mem_kT=np.asarray(L0_attn_mem_k).reshape(HP, 2, MEM, DH).transpose(1, 3, 0, 2).reshape(P, HP * MEM),
        mem_v=np.asarray(L0_attn_mem_v).transpose(1, 0, 2).reshape(MEM, INNER),
        hs_col=pair_cols(np.broadcast_to(head, (H, DH)).reshape(-1)),
        Wg=np.asarray(L0_attn_Wg), bg_col=pair_cols(L0_attn_bg), Wo=np.asarray(L0_attn_Wo),
        WfcT=np.asarray(L0_ffn_W_fc).T,
        lnw_col=np.asarray(L0_ffn_ln_w).reshape(FC, P).T, lnb_col=np.asarray(L0_ffn_ln_b).reshape(FC, P).T,
        WpT=np.asarray(L0_ffn_W_proj).T,
        ident_c=np.eye(P, dtype=np.float32),
        blocks_c=(p[:, None] // DH == p[None, :] // DH).astype(np.float32),
        delta_c=(p[:, None] % R8 == p[None, :] % R8).astype(np.float32),
        mask_c=np.where(u[None, :] - (P - R8) <= p[:, None] % R8, np.float32(0), np.float32(MASKED)),
        guess_c=guess_table(),
    )
    arrays, args = {}, []
    for name, a in layout.items():
        a = np.ascontiguousarray(a)
        arrays[f"in_{name}"] = a
        args.append(nc.dram_tensor(f"in_{name}", a.shape, mybir.dt.from_np(a.dtype), kind="ExternalInput").ap())
    out = nc.dram_tensor("out_x", (B, N, DIM), F32, kind="ExternalOutput").ap()
    build(nc, *args, out)
    r = run_bass_kernel_spmd(nc, [arrays], core_ids=[0])
    return r.results[0]["out_x"]
```
